# Optimizing a Trainium2 kernel written in Bass

```python
import numpy as np
import jax
import jax.numpy as jnp

def _softmax(x, axis=-1):
    return jax.nn.softmax(x, axis=axis)

def _gelu(x):
    return jax.nn.gelu(x, approximate=True)

def _silu(x):
    return jax.nn.silu(x)

def _sigmoid(x):
    return jax.nn.sigmoid(x)

def _layernorm(x, axis=-1, eps=1e-05):
    m = jnp.mean(x, axis=axis, keepdims=True)
    v = jnp.var(x, axis=axis, keepdims=True)
    return (x - m) / jnp.sqrt(v + eps)

def _scatter_add(tgt, idx, src, axis=0):
    return tgt.at[idx].add(src)

def _segment_sum(src, seg, n):
    return jax.ops.segment_sum(src, seg, n)
kernel_name = 'mk_lm_tower_d1_tok_ids256_r4_24edc1'

def setup_inputs(seed: int=0):
    np.random.seed(seed)
    _w = jnp.asarray

    def _rec_inputs():
        import jax
        import jax.numpy as jnp
        _rk = jax.random.key(seed)
        x = jax.random.randint(jax.random.fold_in(_rk, 1), (64, 128), 0, 256, jnp.int32)
        fside_BS_t = jax.random.uniform(jax.random.fold_in(_rk, 21), (64, 128), jnp.float32, 0.0, 0.999994)
        return (x, fside_BS_t)
    x, fside_BS_t = _rec_inputs()

    def _L0_tok_setup():
        import jax, jax.numpy as jnp
        import numpy as np
        NUM_ACTIONS = 256
        EMBED_DIM = 64
        B, T = (64, 1024)
        key = jax.random.key(seed)
        k_a, k_t, k_w = jax.random.split(key, 3)
        actions = jax.random.randint(k_a, (B, T), 0, NUM_ACTIONS, dtype=jnp.int64 if jax.config.jax_enable_x64 else jnp.int32)
        t = jax.random.uniform(k_t, (B, T), dtype=jnp.float32)
        weight = jax.random.normal(k_w, (EMBED_DIM, NUM_ACTIONS), dtype=jnp.float32) * (1.0 / np.sqrt(NUM_ACTIONS))
        return {'actions': actions, 't': t, 'weight': weight}
    _L0_tok_all = _L0_tok_setup()
    _L0_tok_in = {k: v for k, v in _L0_tok_all.items() if k in ('weight',)}
    del _L0_tok_all

    def _L0_attn_setup():
        import jax, jax.numpy as jnp
        import numpy as np
        B, S, F, H = (4, 256, 64, 8)
        SCALE = float(F) ** 0.5
        key = jax.random.key(seed)
        ks = jax.random.split(key, 5)
        return {'q_input': jax.random.normal(ks[0], (B, S, F), dtype=jnp.float32), 'Wq': jax.random.normal(ks[1], (F, F * H), dtype=jnp.float32) * 0.02, 'Wk': jax.random.normal(ks[2], (F, F * H), dtype=jnp.float32) * 0.02, 'Wv': jax.random.normal(ks[3], (F, F * H), dtype=jnp.float32) * 0.02, 'Wo': jax.random.normal(ks[4], (F * H, F), dtype=jnp.float32) * 0.02}
    _L0_attn_all = _L0_attn_setup()
    _L0_attn_in = {k: v for k, v in _L0_attn_all.items() if k in ('Wq', 'Wk', 'Wv', 'Wo')}
    del _L0_attn_all

    def _L0_ffn_setup():
        import jax, jax.numpy as jnp
        import numpy as np
        E, D, H, TOP_K = (6, 64, 64, 2)
        ROUTER_H = D // 2
        key = jax.random.key(seed)
        ks = jax.random.split(key, 12)
        s = 1.0 / np.sqrt(D)
        sh = 1.0 / np.sqrt(H)
        sr = 1.0 / np.sqrt(ROUTER_H)
        return {'features': jax.random.normal(ks[0], (8, 1024, D), dtype=jnp.float32), 'router_w1': jax.random.uniform(ks[1], (D, ROUTER_H), jnp.float32, -s, s), 'router_b1': jnp.zeros((ROUTER_H,), jnp.float32), 'router_w2': jax.random.uniform(ks[2], (ROUTER_H, E), jnp.float32, -sr, sr), 'router_b2': jnp.zeros((E,), jnp.float32), 'expert_w1': jax.random.uniform(ks[3], (E, D, H), jnp.float32, -s, s), 'expert_b1': jnp.zeros((E, H), jnp.float32), 'expert_w2': jax.random.uniform(ks[4], (E, H, H), jnp.float32, -sh, sh), 'expert_b2': jnp.zeros((E, H), jnp.float32), 'expert_w3': jax.random.uniform(ks[5], (E, H, D), jnp.float32, -sh, sh), 'expert_b3': jnp.zeros((E, D), jnp.float32)}
    _L0_ffn_all = _L0_ffn_setup()
    _L0_ffn_in = {k: v for k, v in _L0_ffn_all.items() if k in ('router_w1', 'router_b1', 'router_w2', 'router_b2', 'expert_w1', 'expert_b1', 'expert_w2', 'expert_b2', 'expert_w3', 'expert_b3')}
    del _L0_ffn_all
    return {'x': x, 'fside_BS_t': fside_BS_t, 'L0_tok_weight': _L0_tok_in['weight'], 'L0_attn_Wq': _L0_attn_in['Wq'], 'L0_attn_Wk': _L0_attn_in['Wk'], 'L0_attn_Wv': _L0_attn_in['Wv'], 'L0_attn_Wo': _L0_attn_in['Wo'], 'L0_ffn_router_w1': _L0_ffn_in['router_w1'], 'L0_ffn_router_b1': _L0_ffn_in['router_b1'], 'L0_ffn_router_w2': _L0_ffn_in['router_w2'], 'L0_ffn_router_b2': _L0_ffn_in['router_b2'], 'L0_ffn_expert_w1': _L0_ffn_in['expert_w1'], 'L0_ffn_expert_b1': _L0_ffn_in['expert_b1'], 'L0_ffn_expert_w2': _L0_ffn_in['expert_w2'], 'L0_ffn_expert_b2': _L0_ffn_in['expert_b2'], 'L0_ffn_expert_w3': _L0_ffn_in['expert_w3'], 'L0_ffn_expert_b3': _L0_ffn_in['expert_b3']}

def reference(x, fside_BS_t, L0_tok_weight, L0_attn_Wq, L0_attn_Wk, L0_attn_Wv, L0_attn_Wo, L0_ffn_router_w1, L0_ffn_router_b1, L0_ffn_router_w2, L0_ffn_router_b2, L0_ffn_expert_w1, L0_ffn_expert_b1, L0_ffn_expert_w2, L0_ffn_expert_b2, L0_ffn_expert_w3, L0_ffn_expert_b3):
    import jax
    import jax.numpy as jnp

    def _L0_tok_ref(actions, t, weight):
        import jax, jax.numpy as jnp
        import numpy as np
        NUM_ACTIONS = 256
        EMBED_DIM = 64
        B, T = (64, 1024)
        return jnp.take(weight.T, actions, axis=0)

    def _L0_attn_ref(q_input, Wq, Wk, Wv, Wo):
        import jax, jax.numpy as jnp
        import numpy as np
        B, S, F, H = (4, 256, 64, 8)
        SCALE = float(F) ** 0.5
        b, s, f = q_input.shape
        h = Wq.shape[1] // f
        q = (q_input.reshape(b * s, f) @ Wq).reshape(b, s, f, h)
        k = (q_input.reshape(b * s, f) @ Wk).reshape(b, s, f, h)
        v = (q_input.reshape(b * s, f) @ Wv).reshape(b, s, f, h)
        qkt = jnp.einsum('bifh,bjfh->bijh', q, k)
        attn = jax.nn.sigmoid(qkt * SCALE)
        wv = jnp.einsum('bijh,bjfh->bifh', attn, v)
        wv = wv.reshape(b * s, f * h)
        out = jax.nn.relu(wv @ Wo)
        return out.reshape(b, s, f)

    def _L0_ffn_ref(features, router_w1, router_b1, router_w2, router_b2, expert_w1, expert_b1, expert_w2, expert_b2, expert_w3, expert_b3):
        import jax, jax.numpy as jnp
        import numpy as np
        E, D, H, TOP_K = (6, 64, 64, 2)
        ROUTER_H = D // 2
        rh = jax.nn.relu(features @ router_w1 + router_b1)
        expert_logits = jax.nn.softmax(rh @ router_w2 + router_b2, axis=-1)
        top_w, top_i = jax.lax.top_k(expert_logits, TOP_K)
        routing_weights = jax.nn.softmax(top_w, axis=-1)
        h1 = jax.nn.relu(jnp.einsum('bsd,edh->bseh', features, expert_w1) + expert_b1)
        h2 = jax.nn.relu(jnp.einsum('bseh,ehf->bsef', h1, expert_w2) + expert_b2)
        expert_out = jnp.einsum('bsef,efo->bseo', h2, expert_w3) + expert_b3
        sel = jnp.take_along_axis(expert_out, top_i[:, :, :, None], axis=2)
        combined = jnp.sum(sel * routing_weights[..., None], axis=2)
        return combined
    h = _L0_tok_ref(x, fside_BS_t, L0_tok_weight)
    h = h + _L0_attn_ref(_layernorm(h, axis=-1), L0_attn_Wq, L0_attn_Wk, L0_attn_Wv, L0_attn_Wo)
    h = h + _L0_ffn_ref(_layernorm(h, axis=-1), L0_ffn_router_w1, L0_ffn_router_b1, L0_ffn_router_w2, L0_ffn_router_b2, L0_ffn_expert_w1, L0_ffn_expert_b1, L0_ffn_expert_w2, L0_ffn_expert_b2, L0_ffn_expert_w3, L0_ffn_expert_b3)
    return h

_drawn_inputs = setup_inputs


def setup_inputs(seed=0):
    import zlib

    import numpy as np

    out = dict(_drawn_inputs(seed))
    spreads = {'L0_ffn_router_b1': (0.0, 0.1),
     'L0_ffn_router_b2': (0.0, 0.1),
     'L0_ffn_expert_b1': (0.0, 0.307),
     'L0_ffn_expert_b2': (0.0, 0.1),
     'L0_ffn_expert_b3': (0.0, 0.1)}
    factors = {}
    for name, (base, spread) in spreads.items():
        noise = np.random.default_rng([zlib.crc32(name.encode()), seed]).standard_normal(out[name].shape)
        drawn = base * np.exp(spread * noise) if base else spread * noise
        out[name] = jnp.asarray(drawn.astype(out[name].dtype))
    for name, factor in factors.items():
        out[name] = (out[name] * factor).astype(out[name].dtype)
    return out
```

```python
from contextlib import ExitStack

import concourse.bass as bass
from concourse import mybir

F32 = mybir.dt.float32
F32R = mybir.dt.float32r
BF16 = mybir.dt.bfloat16
I32 = mybir.dt.int32
ALU = mybir.AluOpType
ACT = mybir.ActivationFunctionType
AX = mybir.AxisListType

P = 128
D = 64
HEADS = 8
NV = 256
VK = NV // P
NB = 64
S = 128
E = 6
PAIRS = E // 2
EPS = 1e-5
SCALE = float(D) ** 0.5

CG = 8
NG = NV // CG
FB = 16
NF = D // FB
UG = 8
UNITS = NF * NG // UG
UPF = NG // UG
SP_DMAS, POOL_DMAS = 5, 3
GS_RING, G2_RING, BD_RING = 3, 3, 3
BD_DVE = 5
OB = 4
HEAD_ORDER = (0, 2, 4, 6, 1, 3, 5, 7)
T_BANKS = (2, 3, 4, 0)

TB = 8
STEPS = NB // TB
TOK = TB * S
HT = TOK // 2
RT = 18
LAG = 2
RING = 4

C_ID, C_IOTA, C_MASK, C_SEL, C_BM, C_ROW, C_END = 0, 128, 130, 138, 138 + 192, 334, 334 + 256


def build(nc, x_flat, x_t, consts, tab, wk, wqt, wvt, wo, rw1, rb1, rw2, rb2,
          w1, b1, w2, b2, w3, b3, out):
    vo_dram = nc.dram_tensor("vo_scratch", (NV, HEADS, D), F32, kind="Internal").ap()
    gate_dram = nc.dram_tensor("gate_scratch", (RING, E, TOK), F32, kind="Internal").ap()

    with ExitStack() as ctx:
        def sem(name):
            return ctx.enter_context(nc.semaphore(name))

        def sb(name, shape, dt=F32, where=ctx):
            return where.enter_context(nc.sbuf_tensor(name, shape, dt))

        PS = ctx.enter_context(nc.psum_tensor("PS", [P, 8, 512], F32))

        cst = sb("cst", [P, C_END])
        ident = cst[:, C_ID:C_ID + P]
        table = sb("table", [P, VK, D])
        xt_i = sb("xt_i", [P, NB], I32)
        Htab = sb("Htab", [P, VK, NB, D])
        rb1_s = sb("rb1_s", [P, 1])
        rb2_s = sb("rb2_s", [P, E])
        R1hi, R1lo = sb("R1hi", [P, P], F32R), sb("R1lo", [P, P], F32R)
        R2 = sb("R2", [P, E], F32R)
        W1hi, W1lo = sb("W1hi", [P, E * D], F32R), sb("W1lo", [P, E * D], F32R)
        b1_s, nb2_s = sb("b1_s", [P, PAIRS]), sb("nb2_s", [P, PAIRS])
        W2s = sb("W2s", [P, PAIRS, P])
        W3s = sb("W3s", [P, PAIRS, D])
        BB = sb("BB", [D, 2, D], F32R)
        mhalf = sb("mhalf", [P, TB])

        att = ExitStack()
        w1_raw = sb("w1_raw", [P, E * D], F32, att)
        r1_raw = sb("r1_raw", [P, P], F32, att)
        r2_raw = sb("r2_raw", [P, E], F32, att)
        b2_s = sb("b2_s", [P, PAIRS], F32, att)
        b3_s = sb("b3_s", [D, D], F32, att)
        b3f = sb("b3f", [D, D], F32, att)
        b3hi, b3lo = sb("b3hi", [D, D], F32R, att), sb("b3lo", [D, D], F32, att)
        b3t = sb("b3t", [D, 2, D], F32, att)
        selb2 = sb("selb2", [P, PAIRS, D], F32, att)
        lnt = sb("lnt", [P, 6, VK], F32, att)
        xc0 = sb("xc0", [P, VK, D], F32, att)
        sq0 = sb("sq0", [P, VK, D], F32, att)
        nn0 = sb("nn0", [P, VK, 2, D], F32, att)
        nT = sb("nT", [P, NV], F32, att)
        NDhi, NDlo = sb("NDhi", [P, NV], F32R, att), sb("NDlo", [P, NV], F32R, att)
        xt_f = sb("xt_f", [P, NB], F32, att)
        iota_b = sb("iota_b", [P, NV], BF16, att)
        ones_b = sb("ones_b", [P, 2], BF16, att)
        cnt = sb("cnt", [P, VK, NB], F32, att)
        VOp = sb("VOp", [P, 2, NG, D], F32R, att)
        AH = sb("AH", [P, NG, NV], F32R, att)
        BD = [sb(f"BD{i}", [P, 2, UG, CG, FB], F32R, att) for i in range(BD_RING)]
        Gs = [sb(f"Gs{i}", [P, UG, NV], F32, att) for i in range(GS_RING)]
        O1 = [sb(f"O1{i}", [P, 512], F32, att) for i in range(2)]
        setup = ExitStack()
        wk_s = sb("wk_s", [D, 4, P], F32, setup)
        wqt_s = sb("wqt_s", [P, 4, P], F32, setup)
        wvt_s = sb("wvt_s", [P, 4, D], F32, setup)
        wo_s = sb("wo_s", [P, HEADS, D], F32, setup)
        WVO = sb("WVO", [D, HEADS, D], F32, setup)
        VOs = sb("VOs", [P, VK, HEADS * D], F32, setup)
        VOr = sb("VOr", [P, NG, D], F32, setup)
        kT = sb("kT", [P, 4, NV], F32, setup)
        TS = sb("TS", [P, NG, 2, CG, HEADS], F32R, setup)
        OHt = sb("OHt", [P, 2, OB, NV], BF16, setup)
        As = [sb(f"As{i}", [P, 4, NV], F32, setup) for i in range(2)]
        setup.close()
        G2 = [sb(f"G2{i}", [P, FB, NV], F32, att) for i in range(G2_RING)]
        att.close()

        xb = [sb(f"xb{i}", [P, TOK], I32) for i in range(2)]
        OH = [sb(f"OH{i}", [P, VK, TOK], BF16) for i in range(2)]
        r1 = sb("r1", [P, VK, TB * D])
        r2 = [sb(f"r2{i}", [P, VK, TB * D], BF16) for i in range(2)]
        H2 = [sb(f"H2{i}", [P, TB, D]) for i in range(RING)]
        xc = sb("xc", [P, TB, D])
        sq = sb("sq", [P, TB, D])
        nrm = sb("nrm", [P, TB, D])
        NN = sb("NN", [P, TB, 2, D])
        NNr = sb("NNr", [P, TB, D], F32R)
        st = sb("st", [P, 4, TB])
        X2 = [sb(f"X2{i}", [P, TOK], F32R) for i in range(RING)]
        RF = sb("RF", [P, TOK])
        RH = sb("RH", [P, TOK], F32R)
        lg = sb("lg", [P, TB, E])
        cmp_ = sb("cmp", [P, TB, E, E])
        rank = sb("rank", [P, TB, E])
        m0, m1, sg = (sb(n, [P, TB, E]) for n in ("m0", "m1", "sg"))
        ex, ps_, g0, g1 = (sb(n, [P, TB, E]) for n in ("ex", "ps_", "g0", "g1"))
        gate = sb("gate", [P, TB, E])
        rt = sb("rt", [P, 8, TB])
        GT = [sb(f"GT{i}", [TB * E, P]) for i in range(2)]
        WB = [sb(f"WB{i}", [P, PAIRS, TOK]) for i in range(RING)]
        GG = [sb(f"GG{i}", [D, HT]) for i in range(RING)]
        GP = sb("GP", [D, HT], F32R)
        H1 = [sb(f"H1{q}", [P, TOK]) for q in range(PAIRS)]
        H2g = [sb(f"H2g{q}", [P, TOK]) for q in range(PAIRS)]
        OT = sb("OT", [P, HT])
        Y = [sb(f"Y{i}", [P, TB, D]) for i in range(2)]

        ld_tab, ld_c, ld_x, ld_k, ld_q, ld_v, ld_o = (sem(n) for n in (
            "ld_tab", "ld_c", "ld_x", "ld_k", "ld_q", "ld_v", "ld_o"))
        ld_r, ld_w1, ld_b, ld_w2, ld_w3 = (sem(n) for n in ("ld_r", "ld_w1", "ld_b", "ld_w2", "ld_w3"))
        ln0, ln0_pool, const_ready, nT_ps, nT_sb, nd_hi, nd_lo, x_f, w_hi = (sem(n) for n in (
            "ln0", "ln0_pool", "const_ready", "nT_ps", "nT_sb", "nd_hi", "nd_lo", "x_f", "w_hi"))
        k_ps, k_sb, t_ps, t_hi, t_lo, t_dup = (sem(n) for n in ("k_ps", "k_sb", "t_ps", "t_hi", "t_lo", "t_dup"))
        wvo_ps, wvo_sb, vo_ps, vo_sb, vo_st, vo_ld, vo_hi, vo_ready = (sem(n) for n in (
            "wvo_ps", "wvo_sb", "vo_ps", "vo_sb", "vo_st", "vo_ld", "vo_hi", "vo_ready"))
        oh_ready, cnt_ps, cnt_sb = sem("oh_ready"), sem("cnt_ps"), sem("cnt_sb")
        lg_ps, as_ready, ah_hi, ah_dve, ah_pool = (sem(n) for n in ("lg_ps", "as_ready", "ah_hi", "ah_dve", "ah_pool"))
        w_lo, bias_ps, sel_dve, bias_dve, w2_zero = (sem(n) for n in (
            "w_lo", "bias_ps", "sel_dve", "bias_dve", "w2_zero"))
        bd_dve, bd_act, g_ps, gs_act, gs_dve = (sem(n) for n in ("bd_dve", "bd_act", "g_ps", "gs_act", "gs_dve"))
        sent_sp = [sem(f"sent_sp{i}") for i in range(GS_RING)]
        sent_pool = [sem(f"sent_pool{i}") for i in range(GS_RING)]
        o_ps, o_sb, ot_ps, h_tab = (sem(n) for n in ("o_ps", "o_sb", "ot_ps", "h_tab"))
        x_ld = [sem(f"x_ld{i}") for i in range(2)]
        oh_b, r1_ok, r2_ok, h_ps, h_sb = (sem(n) for n in ("oh_b", "r1_ok", "r2_ok", "h_ps", "h_sb"))
        ln_dve, ln_act, ln_pool, nn_hi, nn_ready = (sem(n) for n in ("ln_dve", "ln_act", "ln_pool", "nn_hi", "nn_ready"))
        x_ps, x_sb, rh_ps, rf_sb, rh_hi, rh_ready = (sem(n) for n in ("x_ps", "x_sb", "rh_ps", "rf_sb", "rh_hi", "rh_ready"))
        rl_ps, rt_dve, ex_act, gate_ready, gt_ps, gt_sb = (sem(n) for n in (
            "rl_ps", "rt_dve", "ex_act", "gate_ready", "gt_ps", "gt_sb"))
        gate_st = [sem(f"gate_st{i}") for i in range(2)]
        wb_ld = [sem(f"wb_ld{i}") for i in range(RING)]
        gg_ld = [sem(f"gg_ld{i}") for i in range(RING)]
        gg_zero, gp_hi, gp_ready = sem("gg_zero"), sem("gp_hi"), sem("gp_ready")
        l1_ps, h1_sb, l2_ps, h2_sb, l3_ps, ot_sb, y_ps, y_sb = (sem(n) for n in (
            "l1_ps", "h1_sb", "l2_ps", "h2_sb", "l3_ps", "ot_sb", "y_ps", "y_sb"))
        y_st = [sem(f"y_st{i}") for i in range(2)]
        cmp_zero = sem("cmp_zero")

        B_G, B_O, B_OT = 0, 4, 6
        B_H, B_X, B_L1, B_L2, B_Y = 0, 1, 3, 5, 7

        def x_load(eng, i):
            eng.dma_start(xb[i % 2][:], x_flat[:, i * TOK:(i + 1) * TOK].broadcast_to([P, TOK]))\
               .then_inc(x_ld[i % 2], 16)

        def send_unit(eng, n, mine, done):
            half = n // 2
            eng.wait_ge(gs_act, 2 * n + 2)
            eng.wait_ge(gs_dve, 2 * n + 2)
            if n == 0:
                eng.wait_ge(ah_dve, 4)
                eng.wait_ge(ah_pool, 4)
                eng.wait_ge(cnt_sb, 1)
                eng.wait_ge(vo_ready, 1)
            if half >= G2_RING and n % 2 == 0:
                eng.wait_ge(o_ps, 4 * ((half - G2_RING) // 2 + 1))
            for m in mine:
                row = (n % 2) * UG + m
                eng.dma_start(G2[half % G2_RING][row * CG:(row + 1) * CG, :, :],
                              Gs[n % GS_RING][:, m, :]).then_inc(done[n % GS_RING], 16)

        def unit_sent(eng, n):
            eng.wait_ge(sent_sp[n % GS_RING], 16 * SP_DMAS * (n // GS_RING + 1))
            eng.wait_ge(sent_pool[n % GS_RING], 16 * POOL_DMAS * (n // GS_RING + 1))

        def table_of(i):
            return Htab[:, :, i * TB:(i + 1) * TB, :].rearrange("p k b f -> p k (b f)")

        def upper(ap):
            return ap.bitcast(BF16).rearrange("p k (n two) -> p k n two", two=2)[:, :, :, 1]

        def two_banks(b):
            return PS[:, b:b + 2, :].rearrange("p b n -> p (b n)")

        def vo_slice(n):
            fg, r = divmod(n, UPF)
            return VOp[:, :, r * UG:(r + 1) * UG, fg * FB:(fg + 1) * FB].bitcast(F32)

        def contraction_after(n):
            fg, r = divmod(n, UPF)
            if fg == 0 or r not in (1, 2):
                return ()
            m = 4 * (fg - 1) + 2 * (r - 1)
            return m, m + 1

        def over(ap, n):
            return ap.unsqueeze(2).broadcast_to([ap.shape[0], ap.shape[1], n])

        def head_pair(ap, b):
            h = HEAD_ORDER[2 * b]
            return ap[:, :, :, h:h + 3:2].rearrange("p g c h -> p h g c")

        block = ctx.enter_context(nc.Block())

        @block.sync
        def _(sp):
            sp.dma_start(table[:], tab.rearrange("(k p) d -> p k d", p=P)).then_inc(ld_tab, 16)
            sp.dma_start(cst[:], consts).then_inc(ld_c, 16)
            sp.dma_start(wk_s[:], wk.rearrange("d (q m) -> d q m", m=P)).then_inc(ld_k, 16)
            sp.dma_start(wqt_s[:], wqt.rearrange("(q p) d -> p q d", p=P)).then_inc(ld_q, 16)
            sp.dma_start(r1_raw[:], rw1).then_inc(ld_r, 16)
            sp.dma_start(r2_raw[:], rw2).then_inc(ld_r, 16)
            sp.dma_start(rb1_s[:], rb1).then_inc(ld_r, 16)
            sp.dma_start(rb2_s[:], rb2.broadcast_to([P, E])).then_inc(ld_r, 16)
            sp.dma_start(w1_raw[:], w1).then_inc(ld_w1, 16)
            sp.wait_ge(vo_sb, VK)
            sp.dma_start(vo_dram.rearrange("(k p) h f -> p k (h f)", p=P), VOs[:]).then_inc(vo_st, 16)
            sp.wait_ge(vo_st, 16)
            for u in range(2):
                sp.dma_start(VOr[u * D:(u + 1) * D, :, :],
                             vo_dram.rearrange("(g c) h f -> (c h) g f", c=CG)).then_inc(vo_ld, 16)
            for n in range(UNITS):
                send_unit(sp, n, range(SP_DMAS), sent_sp)
            for i in range(STEPS + LAG):
                if i < STEPS:
                    if i == 0:
                        sp.wait_ge(o_ps, NF * 4)
                        sp.wait_ge(h_tab, NF * 4 * VK)
                        x_load(sp, 0)
                    if i + 1 < STEPS:
                        if i >= 1:
                            sp.wait_ge(oh_b, VK * i)
                        x_load(sp, i + 1)
                    sp.wait_ge(gt_sb, i + 1)
                    if i >= RING:
                        sp.wait_ge(wb_ld[i % RING], 32 * (i // RING))
                        sp.wait_ge(gg_ld[i % RING], 128 * (i // RING))
                    sp.dma_start(gate_dram[i % RING].rearrange("e (t k) -> t e k", k=S),
                                 GT[i % 2][:]).then_inc(gate_st[i % 2], 16)
                    sp.wait_ge(gate_st[i % 2], 16 * (i // 2 + 1))
                    if i >= RING:
                        sp.wait_ge(h2_sb, PAIRS * (i - RING + 1))
                        sp.wait_ge(gp_ready, i - RING + 1)
                    for e in range(2):
                        src = gate_dram[i % RING].rearrange("(q e) k -> e q k", e=2)[e:e + 1]
                        sp.dma_start(WB[i % RING][e * D:(e + 1) * D, :, :],
                                     src.broadcast_to([D, PAIRS, TOK])).then_inc(wb_ld[i % RING], 16)
                    if i == 0:
                        sp.wait_ge(gg_zero, RING)
                    for w in range(2):
                        for u in range(2):
                            for z in range(2):
                                sp.dma_start(
                                    GG[i % RING][32 * w + 12 * u + 6 * z:32 * w + 12 * u + 6 * z + 6, :],
                                    gate_dram[i % RING][:, u * HT:(u + 1) * HT],
                                ).then_inc(gg_ld[i % RING], 16)
                if i >= LAG:
                    s = i - LAG
                    sp.wait_ge(y_sb, s + 1)
                    sp.dma_start(out[s * TB:(s + 1) * TB].rearrange("t p f -> p t f"),
                                 Y[s % 2][:]).then_inc(y_st[s % 2], 16)
            for i in range(2):
                sp.wait_ge(y_st[i], 16 * (STEPS // 2))

        @block.gpsimd
        def _(pool):
            pool.memset(mhalf[:], -0.5).then_inc(const_ready, 1)
            pool.memset(ones_b[:], 1.0).then_inc(const_ready, 1)
            pool.memset(W2s[:], 0.0).then_inc(w2_zero, 1)
            pool.wait_ge(w2_zero, 1)
            for e in range(2):
                pool.dma_start(W2s[e * D:(e + 1) * D, :, e * D:(e + 1) * D],
                               w2.rearrange("(q e) h f -> e h q f", e=2)[e]).then_inc(ld_w2, 16)
            pool.wait_ge(ln0, 4)
            pool.tensor_scalar(lnt[:, 2, :], lnt[:, 1, :], 1.0 / D, EPS, ALU.mult, ALU.add).then_inc(ln0_pool, 1)
            pool.wait_ge(ln0_pool, 1)
            pool.wait_ge(const_ready, 2)
            pool.tensor_tensor(lnt[:, 3, :], lnt[:, 2, :], mhalf[:, 0:VK], ALU.pow).then_inc(ln0_pool, 1)
            for t in range(1, 8, 2):
                pool.wait_ge(ah_hi, t + 1)
                rows = slice(4 * t, 4 * t + 4)
                pool.tensor_tensor(AH[D:P, rows, :], As[t % 2][D:P], AH[D:P, rows, :].bitcast(F32),
                                   ALU.subtract).then_inc(ah_pool, 1)
            for n in range(UNITS):
                send_unit(pool, n, range(SP_DMAS, UG), sent_pool)

            pool.wait_ge(o_ps, NF * 4)
            pool.wait_ge(h_tab, NF * 4 * VK)
            for i in range(RING):
                pool.memset(GG[i][:], 0.0).then_inc(gg_zero, 1)
            pool.memset(cmp_[:], 0.0).then_inc(cmp_zero, 1)

            def cut(i):
                h = table_of(i)
                if i >= 1:
                    pool.wait_ge(h_ps, i)
                    pool.wait_ge(rh_ready, i)
                pool.tensor_tensor(r1[:], h, upper(h), ALU.subtract).then_inc(r1_ok, 1)
                pool.wait_ge(r1_ok, i + 1)
                pool.tensor_tensor(r2[i % 2][:], r1[:], upper(r1[:]), ALU.subtract).then_inc(r2_ok, 1)

            cut(0)
            for i in range(STEPS):
                pool.wait_ge(ln_dve, 4 * i + 3)
                pool.tensor_scalar(st[:, 2, :], st[:, 1, :], 1.0 / D, EPS, ALU.mult, ALU.add).then_inc(ln_pool, 1)
                pool.wait_ge(ln_pool, 2 * i + 1)
                pool.tensor_tensor(st[:, 3, :], st[:, 2, :], mhalf[:], ALU.pow).then_inc(ln_pool, 1)
                pool.wait_ge(nn_hi, 2 * i + 2)
                pool.tensor_tensor(NN[:, :, 1, :], nrm[:], NNr[:].bitcast(F32), ALU.subtract).then_inc(nn_ready, 1)
                pool.wait_ge(rh_hi, i + 1)
                pool.tensor_tensor(RH[D:P, :], RF[D:P, :], RH[D:P, :].bitcast(F32), ALU.subtract)\
                    .then_inc(rh_ready, 1)
                if i + 1 < STEPS:
                    cut(i + 1)

        @block.scalar
        def _(act):
            act.dma_start(xt_i[:], x_t).then_inc(ld_x, 16)
            act.dma_start(wvt_s[:], wvt.rearrange("(q p) d -> p q d", p=P)).then_inc(ld_v, 16)
            act.dma_start(wo_s[:], wo.rearrange("p (h o) -> p h o", o=D)).then_inc(ld_o, 16)
            act.dma_start(b1_s[:], b1).then_inc(ld_b, 16)
            act.dma_start(b2_s[:], b2).then_inc(ld_b, 16)
            act.dma_start(b3_s[:], b3).then_inc(ld_b, 16)
            act.dma_start(W3s[:], w3.rearrange("(q p) o -> p q o", p=P)).then_inc(ld_w3, 16)
            act.wait_ge(wvo_ps, 1)
            for odd in range(2):
                act.activation(WVO[:, odd::2, :], PS[0:D, 5 + 2 * odd, 0:4 * D].rearrange("p (h o) -> p h o", o=D),
                               ACT.Copy).then_inc(wvo_sb, 1)
            act.wait_ge(nT_ps, 1)
            act.activation(nT[:], PS[:, 6, 0:NV], ACT.Copy).then_inc(nT_sb, 1)
            for b in range(2):
                act.wait_ge(k_ps, b + 1)
                act.activation(kT[:, 2 * b:2 * b + 2, :].rearrange("p q c -> p (q c)"), PS[:, b, :], ACT.Copy)\
                   .then_inc(k_sb, 1)
            for k in range(VK):
                act.wait_ge(vo_ps, k + 1)
                act.activation(VOs[:, k, :], PS[:, 6 + k, :], ACT.Copy).then_inc(vo_sb, 1)
            for b in range(4):
                act.wait_ge(t_ps, b + 1)
                act.activation(head_pair(TS[:, :, 0], b),
                               PS[:, T_BANKS[b], :].rearrange("p (h g c) -> p h g c", h=2, c=CG), ACT.Copy)\
                   .then_inc(t_hi, 1)
            for t in range(8):
                act.wait_ge(lg_ps, t + 1)
                if t >= 2:
                    if t % 2 == 0:
                        act.wait_ge(ah_dve, t // 2)
                    else:
                        act.wait_ge(ah_pool, t // 2)
                b = 2 * (t % 2)
                act.activation(As[t % 2][:].rearrange("p g a -> p (g a)"),
                               PS[:, b:b + 2, :].rearrange("p b n -> p (b n)"), ACT.Sigmoid, scale=SCALE)\
                   .then_inc(as_ready, 1)

            def bd(n):
                if n == 0:
                    act.wait_ge(vo_ready, 1)
                if n >= BD_RING:
                    act.wait_ge(g_ps, 4 * (n - BD_RING + 1))
                for c in range(BD_DVE, CG):
                    ins = act.activation(BD[n % BD_RING][:, :, :, c, :], vo_slice(n), ACT.Copy,
                                         scale=cst[:, C_MASK + c:C_MASK + c + 1])
                ins.then_inc(bd_act, 1)

            def o_evac(m):
                act.wait_ge(o_ps, m + 1)
                if m >= 2:
                    act.wait_ge(ot_ps, m - 1)
                act.activation(O1[m % 2][:], PS[:, B_O + m % 2, :], ACT.Copy).then_inc(o_sb, 1)

            bd(0)
            bd(1)
            for n in range(UNITS):
                if n + 2 < UNITS:
                    bd(n + 2)
                if n >= GS_RING:
                    unit_sent(act, n - GS_RING)
                for j in (0, 2):
                    act.wait_ge(g_ps, 4 * n + j + 1)
                    act.activation(Gs[n % GS_RING][:, 2 * j:2 * j + 2, :].rearrange("p g a -> p (g a)"),
                                   PS[:, B_G + j, :], ACT.Copy).then_inc(gs_act, 1)
                for m in contraction_after(n):
                    o_evac(m)
            for m in range(4 * (NF - 1), 4 * NF):
                o_evac(m)

            def relu1(s, q):
                act.wait_ge(l1_ps, PAIRS * s + q + 1)
                if s >= 1:
                    act.wait_ge(l2_ps, PAIRS * (s - 1) + q + 1)
                act.activation(H1[q][:], two_banks(B_L1), ACT.Relu, bias=b1_s[:, q:q + 1]).then_inc(h1_sb, 1)

            act.wait_ge(ld_b, 48)
            act.wait_ge(ld_r, 64)
            for i in range(STEPS + LAG):
                a, b, s = i < STEPS, i >= LAG, i - LAG
                if a:
                    act.wait_ge(h_ps, i + 1)
                    if i >= RING:
                        act.wait_ge(y_sb, i - RING + 1)
                    act.activation(H2[i % RING][:].rearrange("p t f -> p (t f)"), PS[:, B_H, :], ACT.Copy)\
                       .then_inc(h_sb, 1)
                if b:
                    relu1(s, 0)
                if a:
                    act.wait_ge(ln_dve, 4 * i + 2)
                    act.activation(sq[:], xc[:], ACT.Square).then_inc(ln_act, 1)
                if b:
                    relu1(s, 1)
                if a:
                    act.wait_ge(ln_dve, 4 * i + 4)
                    if i >= 1:
                        act.wait_ge(nn_ready, i)
                        act.wait_ge(x_ps, 2 * i)
                    act.activation(NNr[:], nrm[:], ACT.Copy).then_inc(nn_hi, 1)
                    act.wait_ge(nn_hi, 2 * i + 1)
                    act.activation(NN[:, :, 0, :], NNr[:].bitcast(F32), ACT.Copy).then_inc(nn_hi, 1)
                    act.wait_ge(x_ps, 2 * i + 2)
                    if i >= RING:
                        act.wait_ge(l1_ps, PAIRS * (i - RING + 1))
                    act.activation(X2[i % RING][:], two_banks(B_X), ACT.Copy).then_inc(x_sb, 1)
                if b:
                    relu1(s, 2)
                if a:
                    act.wait_ge(rh_ps, i + 1)
                    if i >= 1:
                        act.wait_ge(rh_ready, i)
                    act.activation(RF[:], two_banks(B_X), ACT.Relu, bias=rb1_s[:, 0:1]).then_inc(rf_sb, 1)
                    act.wait_ge(rf_sb, i + 1)
                    if i >= 1:
                        act.wait_ge(rl_ps, i)
                    act.activation(RH[:], RF[:], ACT.Copy).then_inc(rh_hi, 1)
                    act.wait_ge(rt_dve, RT * i + 3)
                    act.activation(ex[:], ex[:], ACT.Exp).then_inc(ex_act, 1)
                if b:
                    act.wait_ge(l3_ps, s + 1)
                    act.activation(OT[:], PS[:, B_Y, :], ACT.Copy).then_inc(ot_sb, 1)
                if a:
                    act.wait_ge(rt_dve, RT * i + 13)
                    act.activation(rt[:, 4, :], rt[:, 3, :], ACT.Exp, scale=-1.0).then_inc(ex_act, 1)
                    act.wait_ge(gt_ps, i + 1)
                    if i >= 2:
                        act.wait_ge(gate_st[i % 2], 16 * (i // 2))
                    act.activation(GT[i % 2][:], PS[0:TB * E, B_H, 256:256 + P], ACT.Copy).then_inc(gt_sb, 1)

        @block.tensor
        def _(pe):
            pe.wait_ge(ld_v, 16)
            pe.wait_ge(ld_o, 16)
            for h in HEAD_ORDER:
                rows = slice(D * (h % 2), D * (h % 2) + D)
                ins = pe.matmul(PS[0:D, 5 + 2 * (h % 2), h // 2 * D:(h // 2 + 1) * D], wvt_s[rows, h // 2, :],
                                wo_s[rows, h, :], start=True, stop=True)
            ins.then_inc(wvo_ps, 1)
            pe.wait_ge(const_ready, 2)
            pe.wait_ge(wvo_sb, 2)

            def count(a):
                pe.wait_ge(oh_ready, a + 1)
                for b in range(OB):
                    for k in range(VK):
                        c = k * NB + a * OB + b
                        ins = pe.matmul(PS[:, 5, c:c + 1], OHt[:, a % 2, b, k * P:(k + 1) * P],
                                        ones_b[:, 0:1], start=True, stop=True)
                ins.then_inc(cnt_ps, 1)

            count(0)
            count(1)
            pe.wait_ge(ld_c, 16)
            pe.wait_ge(ln0, 6)
            for k in range(VK):
                ins = pe.transpose(PS[:, 6, k * P:(k + 1) * P], nn0[:, k].rearrange("p u d -> p (u d)"), ident)
            ins.then_inc(nT_ps, 1)
            pe.wait_ge(ld_k, 16)
            pe.wait_ge(nT_sb, 1)
            for q in range(4):
                ins = pe.matmul(PS[:, q // 2, (q % 2) * NV:(q % 2 + 1) * NV], wk_s[:, q, :], nT[0:D, :],
                                start=True, stop=True)
                if q % 2:
                    ins.then_inc(k_ps, 1)
            for k in range(VK):
                pe.matmul(PS[:, 6 + k, :], nT[0:D, k * P:(k + 1) * P],
                          WVO[:].rearrange("d h o -> d (h o)"), start=True, stop=True)\
                  .then_inc(vo_ps, 1)
            pe.wait_ge(ld_q, 16)
            pe.wait_ge(k_sb, 2)
            for x, h in enumerate(HEAD_ORDER):
                rows = slice(D * (h % 2), D * (h % 2) + D)
                ins = pe.matmul(PS[:, T_BANKS[x // 2], (x % 2) * NV:(x % 2 + 1) * NV], wqt_s[rows, h // 2, :],
                                kT[rows, h // 2, :], start=True, stop=True)
                if x % 2:
                    ins.then_inc(t_ps, 1)
                count(2 + x)
            for a in range(2 + HEADS, NB // OB):
                count(a)
            pe.wait_ge(sel_dve, 1)
            pe.wait_ge(ld_w3, 16)
            pe.wait_ge(vo_sb, 1)
            for q in range(PAIRS):
                ins = pe.matmul(PS[0:D, 6, 0:D], selb2[:, q, :], W3s[:, q, :], start=(q == 0), stop=(q == 2))
            ins.then_inc(bias_ps, 1)
            pe.wait_ge(nd_lo, 1)
            pe.wait_ge(t_dup, 2)
            for t in range(8):
                if t >= 2:
                    pe.wait_ge(as_ready, t - 1)
                for j in range(4):
                    o = PS[:, 2 * (t % 2) + j // 2, (j % 2) * NV:(j % 2 + 1) * NV]
                    w = TS[:, 4 * t + j].rearrange("p u c h -> p (u c h)")
                    pe.matmul(o, w, NDhi[:], start=True, stop=False)
                    ins = pe.matmul(o, w, NDlo[:], start=False, stop=True)
                ins.then_inc(lg_ps, 1)

            def unit(n):
                pe.wait_ge(bd_dve, n + 1)
                pe.wait_ge(bd_act, n + 1)
                r = n % UPF
                for j in range(4):
                    if n == 0 and j == 0:
                        pe.wait_ge(as_ready, 8)
                    if r < 4 and n < UPF and j % 2 == 0:
                        t = 2 * r + j // 2
                        pe.wait_ge(ah_pool if t % 2 else ah_dve, t // 2 + 1)
                    if n >= 1:
                        pe.wait_ge(gs_dve if j % 2 else gs_act, 2 * (n - 1) + j // 2 + 1)
                    for m in range(2):
                        gl = 2 * j + m
                        o = PS[:, B_G + j, m * NV:(m + 1) * NV]
                        for part in range(2):
                            ins = pe.matmul(o, BD[n % BD_RING][:, part, gl].rearrange("p c f -> p (c f)"),
                                            AH[:, r * UG + gl, :], start=(part == 0), stop=(part == 1))
                    ins.then_inc(g_ps, 1)

            def contract(m):
                fg, j = divmod(m, 4)
                if m == 0:
                    pe.wait_ge(cnt_sb, 1)
                    pe.wait_ge(bias_dve, 1)
                if j == 0:
                    for n in range(UPF * fg, UPF * (fg + 1)):
                        unit_sent(pe, n)
                if m >= 2:
                    pe.wait_ge(o_sb, m - 1)
                for k in range(VK):
                    for u in range(2):
                        f = (FB // 2) * u + 2 * j
                        ins = pe.matmul(PS[u * NB:(u + 1) * NB, B_O + m % 2, :], cnt[:, k, :],
                                        G2[(2 * fg + k) % G2_RING][:, f:f + 2, :].rearrange("p f a -> p (f a)"),
                                        start=(k == 0), stop=(k == 1), skip_group_check=True)
                ins.then_inc(o_ps, 1)

            def turn(m):
                pe.wait_ge(o_sb, m + 1)
                if m >= 2:
                    pe.wait_ge(h_tab, VK * (m - 1))
                for x in range(4):
                    ins = pe.transpose(PS[:, B_OT + m % 2, x * P:(x + 1) * P], O1[m % 2][:, x * P:(x + 1) * P], ident)
                ins.then_inc(ot_ps, 1)

            for n in range(UNITS):
                unit(n)
                for m in contraction_after(n):
                    contract(m)
                    if m >= 1:
                        turn(m - 1)
            for m in range(4 * (NF - 1), 4 * NF):
                contract(m)
                turn(m - 1)
            turn(4 * NF - 1)

            def gather(i):
                pe.wait_ge(oh_b, VK * (i + 1))
                pe.wait_ge(r2_ok, i + 1)
                if i == 0:
                    pe.wait_ge(h_tab, NF * 4 * VK)
                if i >= 1:
                    pe.wait_ge(gt_sb, i)
                parts = (upper(table_of(i)), upper(r1[:]), r2[i % 2][:])
                for t in range(TB):
                    for k in range(VK):
                        for x, part in enumerate(parts):
                            ins = pe.matmul(PS[:, B_H, t * D:(t + 1) * D], OH[i % 2][:, k, t * S:(t + 1) * S],
                                            part[:, k, t * D:(t + 1) * D], start=(k == 0 and x == 0),
                                            stop=(k == 1 and x == 2))
                ins.then_inc(h_ps, 1)

            def turn_rows(i):
                pe.wait_ge(nn_hi, 2 * i + 2)
                pe.wait_ge(nn_ready, i + 1)
                if i >= 1:
                    pe.wait_ge(rf_sb, i)
                for t in range(TB):
                    ins = pe.transpose(PS[:, B_X + t // 4, (t % 4) * P:(t % 4 + 1) * P],
                                       NN[:, t].rearrange("p u d -> p (u d)"), ident)
                    if t % 4 == 3:
                        ins.then_inc(x_ps, 1)

            def hidden(i):
                pe.wait_ge(x_sb, i + 1)
                if i == 0:
                    pe.wait_ge(w_lo, 4)
                for part, w in enumerate((R1hi, R1lo)):
                    for u in range(2):
                        ins = pe.matmul(PS[:, B_X + u, :], w[:], X2[i % RING][:, u * HT:(u + 1) * HT],
                                        start=(part == 0), stop=(part == 1), skip_group_check=True)
                ins.then_inc(rh_ps, 1)

            def router(i):
                pe.wait_ge(rh_ready, i + 1)
                pe.wait_ge(h_sb, i + 1)
                for t in range(TB):
                    ins = pe.matmul(PS[:, B_H, t * E:(t + 1) * E], RH[:, t * P:(t + 1) * P], R2[:],
                                    start=True, stop=True)
                ins.then_inc(rl_ps, 1)

            def turn_gates(i):
                pe.wait_ge(gate_ready, i + 1)
                pe.transpose(PS[0:TB * E, B_H, 256:256 + P], gate[:].rearrange("p t e -> p (t e)"), ident)\
                  .then_inc(gt_ps, 1)

            def layer1(s, q):
                if PAIRS * s + q >= 1:
                    pe.wait_ge(h1_sb, PAIRS * s + q)
                for part, w in enumerate((W1hi, W1lo)):
                    for u in range(2):
                        ins = pe.matmul(PS[:, B_L1 + u, :], w[:, q * P:(q + 1) * P],
                                        X2[s % RING][:, u * HT:(u + 1) * HT], start=(part == 0), stop=(part == 1),
                                        skip_group_check=True)
                ins.then_inc(l1_ps, 1)

            def layer2(s, q):
                pe.wait_ge(h1_sb, PAIRS * s + q + 1)
                if s == 0 and q == 0:
                    pe.wait_ge(ld_w2, 32)
                if PAIRS * s + q >= 1:
                    pe.wait_ge(h2_sb, PAIRS * s + q)
                for u in range(2):
                    ins = pe.matmul(PS[:, B_L2 + u, :], W2s[:, q, :], H1[q][:, u * HT:(u + 1) * HT],
                                    start=True, stop=True)
                ins.then_inc(l2_ps, 1)

            def layer3(s):
                pe.wait_ge(gp_ready, s + 1)
                if s >= 1:
                    pe.wait_ge(y_sb, s)
                pe.matmul(PS[:, B_Y, :], BB[:].rearrange("p u o -> p (u o)"), GP[:], start=True, stop=False,
                          skip_group_check=True)
                for q in range(PAIRS):
                    pe.wait_ge(h2_sb, PAIRS * s + q + 1)
                    for u in range(2):
                        ins = pe.matmul(PS[u * D:(u + 1) * D, B_Y, :], W3s[:, q, :], H2g[q][:, u * HT:(u + 1) * HT],
                                        start=False, stop=(q == PAIRS - 1), skip_group_check=True)
                ins.then_inc(l3_ps, 1)

            def turn_out(s):
                pe.wait_ge(ot_sb, s + 1)
                for j in range(4):
                    ins = pe.transpose(PS[:, B_Y, j * P:(j + 1) * P], OT[:, j * P:(j + 1) * P], ident)
                ins.then_inc(y_ps, 1)

            for i in range(STEPS + LAG):
                a, b, s = i < STEPS, i >= LAG, i - LAG
                if a:
                    gather(i)
                if b:
                    layer1(s, 0)
                    layer1(s, 1)
                    layer2(s, 0)
                if a:
                    turn_rows(i)
                if b:
                    layer1(s, 2)
                    layer2(s, 1)
                if a:
                    hidden(i)
                if b:
                    layer2(s, 2)
                if a:
                    router(i)
                if b:
                    layer3(s)
                    turn_out(s)
                if a:
                    turn_gates(i)

        @block.vector
        def _(dve):
            dve.wait_ge(ld_tab, 16)
            dve.tensor_reduce(lnt[:, 0, :], table[:], AX.X, ALU.add).then_inc(ln0, 1)
            dve.wait_ge(ln0, 1)
            dve.scalar_tensor_tensor(out=xc0[:], in0=lnt[:, 0, :].unsqueeze(2).broadcast_to([P, VK, D]),
                                     scalar=-1.0 / D, in1=table[:], op0=ALU.mult, op1=ALU.add).then_inc(ln0, 1)
            dve.wait_ge(ln0, 2)
            dve.tensor_tensor(sq0[:], xc0[:], xc0[:], ALU.mult).then_inc(ln0, 1)
            dve.wait_ge(ln0, 3)
            dve.tensor_reduce(lnt[:, 1, :], sq0[:], AX.X, ALU.add).then_inc(ln0, 1)
            dve.wait_ge(ld_c, 16)
            dve.wait_ge(ld_x, 16)
            dve.tensor_copy(iota_b[:], cst[:, C_ROW:C_ROW + NV]).then_inc(x_f, 1)
            dve.tensor_copy(xt_f[:], xt_i[:]).then_inc(x_f, 1)
            dve.wait_ge(x_f, 2)

            def one_hots(a):
                if a >= 2:
                    dve.wait_ge(cnt_ps, a - 1)
                for b in range(OB):
                    ins = dve.tensor_scalar(OHt[:, a % 2, b, :], iota_b[:], xt_f[:, OB * a + b:OB * a + b + 1],
                                            None, ALU.is_equal)
                ins.then_inc(oh_ready, 1)

            one_hots(0)
            one_hots(1)
            dve.wait_ge(ln0_pool, 2)
            for u in range(2):
                dve.tensor_tensor(nn0[:, :, u, :], xc0[:], lnt[:, 3, :].unsqueeze(2).broadcast_to([P, VK, D]),
                                  ALU.mult).then_inc(ln0, 1)
            dve.wait_ge(nT_sb, 1)
            dve.tensor_copy(NDhi[:], nT[:]).then_inc(nd_hi, 1)
            dve.wait_ge(nd_hi, 1)
            dve.tensor_tensor(NDlo[:], nT[:], NDhi[:].bitcast(F32), ALU.subtract).then_inc(nd_lo, 1)
            for a in range(2, NB // OB - 4):
                one_hots(a)
            dve.wait_ge(ld_b, 48)
            for q in range(PAIRS):
                ins = dve.tensor_scalar(selb2[:, q, :], cst[:, C_SEL + q * D:C_SEL + (q + 1) * D], b2_s[:, q:q + 1],
                                        None, ALU.mult)
            ins.then_inc(sel_dve, 1)
            dve.tensor_scalar(nb2_s[:], b2_s[:], -1.0, None, ALU.mult).then_inc(sel_dve, 1)
            for b in range(4):
                dve.wait_ge(t_hi, b + 1)
                v = head_pair(TS[D:P, :, 0], b)
                dve.tensor_tensor(v, PS[D:P, T_BANKS[b], :].rearrange("p (h g c) -> p h g c", h=2, c=CG),
                                  v.bitcast(F32), ALU.subtract).then_inc(t_lo, 1)
                one_hots(NB // OB - 4 + b)
            dve.wait_ge(t_lo, 4)
            for x in range(2):
                g = slice(x * NG // 2, (x + 1) * NG // 2)
                dve.tensor_copy(TS[:, g, 1], TS[:, g, 0].bitcast(F32)).then_inc(t_dup, 1)
            dve.wait_ge(cnt_ps, NB // OB)
            dve.tensor_copy(cnt[:].rearrange("p k b -> p (k b)"), PS[:, 5, 0:VK * NB]).then_inc(cnt_sb, 1)
            for t in range(8):
                rows = slice(4 * t, 4 * t + 4)
                dve.wait_ge(as_ready, t + 1)
                dve.tensor_copy(AH[:, rows, :], As[t % 2][:]).then_inc(ah_hi, 1)
                if t % 2 == 0:
                    dve.wait_ge(ah_hi, t + 1)
                    dve.tensor_tensor(AH[D:P, rows, :], As[t % 2][D:P], AH[D:P, rows, :].bitcast(F32),
                                      ALU.subtract).then_inc(ah_dve, 1)
                if t == 1:
                    dve.wait_ge(vo_ld, 32)
                    dve.tensor_copy(VOp[:, 0], VOr[:]).then_inc(vo_hi, 1)
                if t == 2:
                    dve.wait_ge(vo_hi, 1)
                    dve.tensor_tensor(VOp[:, 1], VOr[:], VOp[:, 0].bitcast(F32), ALU.subtract).then_inc(vo_ready, 1)

            def bd(n):
                if n == 0:
                    dve.wait_ge(vo_ready, 1)
                if n >= BD_RING:
                    dve.wait_ge(g_ps, 4 * (n - BD_RING + 1))
                for c in range(BD_DVE):
                    ins = dve.tensor_scalar(BD[n % BD_RING][:, :, :, c, :], vo_slice(n),
                                            cst[:, C_MASK + c:C_MASK + c + 1], None, ALU.mult)
                ins.then_inc(bd_dve, 1)

            def table_rows(m):
                fg, j = divmod(m, 4)
                dve.wait_ge(ot_ps, m + 1)
                for k in range(VK):
                    f0 = fg * FB + 2 * j
                    o = Htab[:, k].rearrange("p b (f2 u f) -> p f2 u f b", u=2, f=FB // 2)[:, fg, :, 2 * j:2 * j + 2, :]
                    e = table[:, k].rearrange("p (f2 u f) -> p f2 u f", u=2, f=FB // 2)[:, fg, :, 2 * j:2 * j + 2]
                    for f in range(2):
                        src = PS[:, B_OT + m % 2, (2 * f + k) * P:(2 * f + k + 1) * P].rearrange(
                            "p (u b) -> p u b", u=2)
                        ins = dve.scalar_tensor_tensor(
                            out=o[:, :, f, :], in0=src, scalar=0.0,
                            in1=e[:, :, f].unsqueeze(2).broadcast_to([P, 2, NB]), op0=ALU.max, op1=ALU.add)
                    ins.then_inc(h_tab, 1)

            def mixture_weights(n):
                if n == 0:
                    dve.wait_ge(bias_ps, 1)
                    dve.tensor_tensor(b3f[:], PS[0:D, 6, 0:D], b3_s[:], ALU.add).then_inc(bias_dve, 1)
                    dve.wait_ge(bias_dve, 1)
                    dve.tensor_copy(b3hi[:], b3f[:]).then_inc(bias_dve, 1)
                    dve.wait_ge(ld_r, 64)
                    dve.tensor_copy(R1hi[:], r1_raw[:]).then_inc(w_hi, 1)
                    dve.tensor_copy(R2[:], r2_raw[:]).then_inc(w_hi, 1)
                    dve.wait_ge(ld_w1, 16)
                    dve.tensor_copy(W1hi[:], w1_raw[:]).then_inc(w_hi, 1)
                if n == 1:
                    dve.wait_ge(bias_dve, 2)
                    dve.tensor_tensor(b3lo[:], b3f[:], b3hi[:].bitcast(F32), ALU.subtract).then_inc(bias_dve, 1)
                    for u in range(2):
                        dve.tensor_scalar(b3t[:, u, :], b3hi[:].bitcast(F32), cst[0:D, C_BM + u:C_BM + u + 1], None,
                                          ALU.mult).then_inc(bias_dve, 1)
                    dve.wait_ge(w_hi, 3)
                    dve.tensor_tensor(R1lo[:], r1_raw[:], R1hi[:].bitcast(F32), ALU.subtract).then_inc(w_lo, 1)
                    for r in (32, 96):
                        dve.tensor_tensor(R2[r:r + 32], r2_raw[r:r + 32], R2[r:r + 32].bitcast(F32), ALU.subtract)\
                           .then_inc(w_lo, 1)
                    dve.tensor_tensor(W1lo[:], w1_raw[:], W1hi[:].bitcast(F32), ALU.subtract).then_inc(w_lo, 1)
                if n == 2:
                    dve.wait_ge(bias_dve, 5)
                    for u in range(2):
                        dve.scalar_tensor_tensor(out=BB[:, u, :], in0=b3lo[:],
                                                 scalar=cst[0:D, C_BM + 2 + u:C_BM + 3 + u], in1=b3t[:, u, :],
                                                 op0=ALU.mult, op1=ALU.add).then_inc(bias_dve, 1)

            bd(0)
            bd(1)
            for n in range(UNITS):
                if n + 2 < UNITS:
                    bd(n + 2)
                mixture_weights(n)
                if n >= GS_RING:
                    unit_sent(dve, n - GS_RING)
                for j in (1, 3):
                    dve.wait_ge(g_ps, 4 * n + j + 1)
                    dve.tensor_copy(Gs[n % GS_RING][:, 2 * j:2 * j + 2, :].rearrange("p g a -> p (g a)"),
                                    PS[:, B_G + j, :]).then_inc(gs_dve, 1)
                for m in contraction_after(n):
                    if m >= 1:
                        table_rows(m - 1)
            for m in range(4 * (NF - 1) - 1, 4 * NF):
                table_rows(m)

            def one_hot_ids(i):
                dve.wait_ge(x_ld[i % 2], 16 * (i // 2 + 1))
                if i >= 2:
                    dve.wait_ge(h_ps, i - 1)
                for k in range(VK):
                    dve.tensor_scalar(OH[i % 2][:, k, :], xb[i % 2][:], cst[:, C_IOTA + k:C_IOTA + k + 1], None,
                                      ALU.is_equal).then_inc(oh_b, 1)

            def centre(i):
                dve.wait_ge(h_sb, i + 1)
                dve.tensor_reduce(st[:, 0, :], H2[i % RING][:], AX.X, ALU.add).then_inc(ln_dve, 1)
                dve.wait_ge(ln_dve, 4 * i + 1)
                dve.scalar_tensor_tensor(out=xc[:], in0=over(st[:, 0, :], D), scalar=-1.0 / D,
                                         in1=H2[i % RING][:], op0=ALU.mult, op1=ALU.add).then_inc(ln_dve, 1)

            def normalise(i):
                dve.wait_ge(ln_act, i + 1)
                dve.tensor_reduce(st[:, 1, :], sq[:], AX.X, ALU.add).then_inc(ln_dve, 1)
                dve.wait_ge(ln_pool, 2 * i + 2)
                if i >= 1:
                    dve.wait_ge(nn_ready, i)
                dve.tensor_tensor(nrm[:], xc[:], over(st[:, 3, :], D), ALU.mult).then_inc(ln_dve, 1)

            def gate2(s, q):
                dve.wait_ge(l2_ps, PAIRS * s + q + 1)
                if q == 0:
                    dve.wait_ge(wb_ld[s % RING], 32 * (s // RING + 1))
                if s >= 1 and q == 0:
                    dve.wait_ge(l3_ps, s)
                dve.scalar_tensor_tensor(out=H2g[q][:], in0=two_banks(B_L2), scalar=nb2_s[:, q:q + 1],
                                         in1=WB[s % RING][:, q, :], op0=ALU.max, op1=ALU.mult).then_inc(h2_sb, 1)

            def gate_parts(s):
                dve.wait_ge(gg_ld[s % RING], 128 * (s // RING + 1))
                if s >= 1:
                    dve.wait_ge(l3_ps, s)
                dve.tensor_copy(GP[:], GG[s % RING][:]).then_inc(gp_hi, 1)
                dve.wait_ge(gp_hi, s + 1)
                dve.tensor_tensor(GP[32:D], GG[s % RING][32:D], GP[32:D].bitcast(F32), ALU.subtract)\
                   .then_inc(gp_ready, 1)

            def route(i):
                n = [RT * i]

                def then(ins):
                    n[0] += 1
                    ins.then_inc(rt_dve, 1)
                    dve.wait_ge(rt_dve, n[0])

                if i == 0:
                    dve.wait_ge(cmp_zero, 1)
                dve.wait_ge(rl_ps, i + 1)
                then(dve.tensor_tensor(lg[:], PS[:, B_H, 0:TB * E].rearrange("p (t e) -> p t e", e=E),
                                       rb2_s[:].unsqueeze(1).broadcast_to([P, TB, E]), ALU.add))
                then(dve.tensor_reduce(rt[:, 0, :], lg[:], AX.X, ALU.max))
                then(dve.tensor_tensor(ex[:], lg[:], over(rt[:, 0, :], E), ALU.subtract))
                for e in range(E):
                    if e > 0:
                        last = dve.tensor_tensor(cmp_[:, :, e, 0:e], lg[:, :, 0:e], over(lg[:, :, e], e), ALU.is_ge)
                    if e < E - 1:
                        last = dve.tensor_tensor(cmp_[:, :, e, e + 1:E], lg[:, :, e + 1:E],
                                                 over(lg[:, :, e], E - 1 - e), ALU.is_gt)
                then(last)
                then(dve.tensor_reduce(rank[:], cmp_[:], AX.X, ALU.add))
                then(dve.tensor_scalar(m0[:], rank[:], 0.0, None, ALU.is_equal))
                then(dve.tensor_scalar(m1[:], rank[:], 1.0, None, ALU.is_equal))
                then(dve.tensor_tensor(sg[:], m0[:], m1[:], ALU.subtract))
                dve.wait_ge(ex_act, 2 * i + 1)
                then(dve.tensor_reduce(rt[:, 1, :], ex[:], AX.X, ALU.add))
                then(dve.tensor_tensor(ps_[:], ex[:], sg[:], ALU.mult))
                then(dve.tensor_reduce(rt[:, 2, :], ps_[:], AX.X, ALU.add))
                then(dve.reciprocal(rt[:, 5, :], rt[:, 1, :]))
                then(dve.tensor_tensor(rt[:, 3, :], rt[:, 2, :], rt[:, 5, :], ALU.mult))
                dve.wait_ge(ex_act, 2 * i + 2)
                then(dve.tensor_scalar(rt[:, 6, :], rt[:, 4, :], 1.0, None, ALU.add))
                then(dve.reciprocal(rt[:, 7, :], rt[:, 6, :]))
                then(dve.tensor_tensor(rt[:, 5, :], rt[:, 4, :], rt[:, 7, :], ALU.mult))
                then(dve.tensor_tensor(g0[:], m0[:], over(rt[:, 7, :], E), ALU.mult))
                then(dve.tensor_tensor(g1[:], m1[:], over(rt[:, 5, :], E), ALU.mult))
                if i >= 1:
                    dve.wait_ge(gt_ps, i)
                dve.tensor_tensor(gate[:], g0[:], g1[:], ALU.add).then_inc(gate_ready, 1)

            def result(s):
                dve.wait_ge(y_ps, s + 1)
                if s >= 2:
                    dve.wait_ge(y_st[s % 2], 16 * (s // 2))
                dve.tensor_tensor(Y[s % 2][:].rearrange("p (u j) o -> p u j o", u=2),
                                  PS[:, B_Y, :].rearrange("p (j u o) -> p u j o", u=2, o=D),
                                  H2[s % RING][:].rearrange("p (u j) o -> p u j o", u=2), ALU.add).then_inc(y_sb, 1)

            one_hot_ids(0)
            dve.wait_ge(sel_dve, 2)
            for i in range(STEPS + LAG):
                a, b, s = i < STEPS, i >= LAG, i - LAG
                if a:
                    centre(i)
                if b:
                    gate2(s, 0)
                if a:
                    normalise(i)
                if b:
                    gate2(s, 1)
                    gate_parts(s)
                    gate2(s, 2)
                if a:
                    route(i)
                if b:
                    result(s)
                if i + 1 < STEPS:
                    one_hot_ids(i + 1)

_NAMES = ("x_flat", "x_t", "consts", "tab", "wk", "wqt", "wvt", "wo", "rw1", "rb1", "rw2", "rb2",
          "w1", "b1", "w2", "b2", "w3", "b3")


def shape_constants():
    import numpy as np

    c = np.zeros((P, C_END), np.float32)
    p = np.arange(P)
    c[:, C_ID:C_ID + P] = np.eye(P)
    for k in range(VK):
        c[:, C_IOTA + k] = p + k * P
    c[p, C_MASK + (p // HEADS) % CG] = 1
    for w in range(2):
        for u in range(2):
            for z in range(2):
                for e in range(E):
                    row = 32 * w + 12 * u + 6 * z + e
                    c[(e % 2) * D:(e % 2 + 1) * D, C_SEL + (e // 2) * D + row] = 1
                    c[row, C_BM + 2 * z + u] = 1
    c[:, C_ROW:C_ROW + NV] = np.arange(NV)
    return c


def kernel(x, fside_BS_t, L0_tok_weight, L0_attn_Wq, L0_attn_Wk, L0_attn_Wv, L0_attn_Wo,
           L0_ffn_router_w1, L0_ffn_router_b1, L0_ffn_router_w2, L0_ffn_router_b2,
           L0_ffn_expert_w1, L0_ffn_expert_b1, L0_ffn_expert_w2, L0_ffn_expert_b2,
           L0_ffn_expert_w3, L0_ffn_expert_b3):
    import numpy as np
    from concourse import bacc
    from concourse.bass_utils import run_bass_kernel_spmd

    x = np.asarray(x)
    head_rows = {n: np.asarray(w).reshape(D, D, HEADS).transpose(2, 1, 0).reshape(HEADS * D, D)
                 for n, w in (("q", L0_attn_Wq), ("v", L0_attn_Wv))}
    wo = np.asarray(L0_attn_Wo).reshape(D, HEADS * D)
    b3_rows = np.zeros((D, D), np.asarray(L0_ffn_expert_b3).dtype)
    for w in range(2):
        for k in range(4):
            b3_rows[32 * w + 6 * k:32 * w + 6 * k + E] = np.asarray(L0_ffn_expert_b3)
    w1 = np.asarray(L0_ffn_expert_w1).transpose(1, 0, 2).reshape(D, E * D)
    arrays = {
        "x_flat": x.reshape(1, NB * S),
        "x_t": x.T,
        "consts": shape_constants(),
        "tab": np.asarray(L0_tok_weight).T,
        "wk": np.asarray(L0_attn_Wk).reshape(D, D, HEADS).transpose(0, 2, 1).reshape(D, HEADS * D),
        "wqt": np.concatenate([head_rows["q"]] * 2, axis=1),
        "wvt": head_rows["v"],
        "wo": np.concatenate([wo, wo]),
        "rw1": np.tile(np.asarray(L0_ffn_router_w1), (2, 4)),
        "rb1": np.tile(np.asarray(L0_ffn_router_b1), 4).reshape(P, 1),
        "rw2": np.tile(np.asarray(L0_ffn_router_w2), (4, 1)),
        "rb2": np.asarray(L0_ffn_router_b2).reshape(1, E),
        "w1": np.concatenate([w1, w1]),
        "b1": np.asarray(L0_ffn_expert_b1).reshape(PAIRS, P).T,
        "w2": np.asarray(L0_ffn_expert_w2),
        "b2": np.asarray(L0_ffn_expert_b2).reshape(PAIRS, P).T,
        "w3": np.asarray(L0_ffn_expert_w3).reshape(E * D, D),
        "b3": b3_rows,
    }
    nc = bacc.Bacc("TRN2", target_bir_lowering=False, num_devices=1)
    args = []
    for name in _NAMES:
        arrays[name] = np.ascontiguousarray(arrays[name])
        args.append(nc.dram_tensor(name, arrays[name].shape, mybir.dt.from_np(arrays[name].dtype),
                                   kind="ExternalInput").ap())
    out = nc.dram_tensor("h_out", (NB, S, D), F32, kind="ExternalOutput").ap()
    build(nc, *args, out)
    result = run_bass_kernel_spmd(nc, [arrays], core_ids=[0])
    return result.results[0]["h_out"]
```

```python
from contextlib import ExitStack

import concourse.bass as bass
from concourse import mybir

F32 = mybir.dt.float32
F32R = mybir.dt.float32r
BF16 = mybir.dt.bfloat16
I32 = mybir.dt.int32
ALU = mybir.AluOpType
ACT = mybir.ActivationFunctionType
AX = mybir.AxisListType

P = 128
D = 64
HEADS = 8
NV = 256
VK = NV // P
NB = 64
S = 128
E = 6
PAIRS = E // 2
EPS = 1e-5
SCALE = float(D) ** 0.5

CG = 8
NG = NV // CG
FB = 16
NF = D // FB
UG = 8
UNITS = NF * NG // UG
UPF = NG // UG
SP_DMAS, POOL_DMAS = 5, 3
GS_RING, G2_RING, BD_RING = 2, 4, 3
BD_DVE = 5
VO_AT = 3
OH_EARLY = 8
OB = 4
HEAD_ORDER = (0, 2, 4, 6, 1, 3, 5, 7)
T_BANKS = (2, 3, 4, 0)

TB = 8
STEPS = NB // TB
TOK = TB * S
HT = TOK // 2
RT = 18
LAG = 2
RING = 4
H_RING = 5

C_ID, C_IOTA, C_MASK, C_SEL, C_BM, C_ROW, C_END = 0, 128, 130, 138, 138 + 192, 334, 334 + 256


def build(nc, x_flat, x_t, consts, tab, wk, wqt, wvt, wo, rw1, rb1, rw2, rb2,
          w1, b1, w2, b2, w3, b3, out):
    vo_dram = nc.dram_tensor("vo_scratch", (NV, HEADS, D), F32, kind="Internal").ap()
    gate_dram = nc.dram_tensor("gate_scratch", (RING, E, TOK), F32, kind="Internal").ap()

    with ExitStack() as ctx:
        def sem(name):
            return ctx.enter_context(nc.semaphore(name))

        def sb(name, shape, dt=F32, where=ctx):
            return where.enter_context(nc.sbuf_tensor(name, shape, dt))

        PS = ctx.enter_context(nc.psum_tensor("PS", [P, 8, 512], F32))

        cst = sb("cst", [P, C_END])
        ident = cst[:, C_ID:C_ID + P]
        table = sb("table", [P, VK, D])
        xt_i = sb("xt_i", [P, NB], I32)
        Htab = sb("Htab", [P, VK, NB, D])
        rb1_s = sb("rb1_s", [P, 1])
        rb2_s = sb("rb2_s", [P, E])
        R1hi, R1lo = sb("R1hi", [P, P], F32R), sb("R1lo", [P, P], F32R)
        R2 = sb("R2", [P, E], F32R)
        W1hi, W1lo = sb("W1hi", [P, E * D], F32R), sb("W1lo", [P, E * D], F32R)
        b1_s, nb2_s = sb("b1_s", [P, PAIRS]), sb("nb2_s", [P, PAIRS])
        W2s = sb("W2s", [P, PAIRS, P])
        W3s = sb("W3s", [P, PAIRS, D])
        BB = sb("BB", [D, 2, D], F32R)
        mhalf = sb("mhalf", [P, TB])

        att = ExitStack()
        w1_raw = sb("w1_raw", [P, E * D], F32, att)
        r1_raw = sb("r1_raw", [P, P], F32, att)
        r2_raw = sb("r2_raw", [P, E], F32, att)
        b2_s = sb("b2_s", [P, PAIRS], F32, att)
        b3_s = sb("b3_s", [D, D], F32, att)
        b3f = sb("b3f", [D, D], F32, att)
        b3hi, b3lo = sb("b3hi", [D, D], F32R, att), sb("b3lo", [D, D], F32, att)
        b3t = sb("b3t", [D, 2, D], F32, att)
        selb2 = sb("selb2", [P, PAIRS, D], F32, att)
        lnt = sb("lnt", [P, 6, VK], F32, att)
        nT = sb("nT", [P, NV], F32, att)
        NDhi, NDlo = sb("NDhi", [P, NV], F32R, att), sb("NDlo", [P, NV], F32R, att)
        xt_f = sb("xt_f", [P, NB], F32, att)
        iota_b = sb("iota_b", [P, NV], BF16, att)
        ones_b = sb("ones_b", [P, 2], BF16, att)
        cnt = sb("cnt", [P, VK, NB], F32, att)
        VOp = sb("VOp", [P, 2, NG, D], F32R, att)
        AH = sb("AH", [P, NG, NV], F32R, att)
        BD = [sb(f"BD{i}", [P, 2, UG, CG, FB], F32R, att) for i in range(BD_RING)]
        Gs = [sb(f"Gs{i}", [P, UG, NV], F32, att) for i in range(GS_RING)]
        O1 = [sb(f"O1{i}", [P, 512], F32, att) for i in range(2)]
        setup = ExitStack()
        xc0 = sb("xc0", [P, VK, D], F32, setup)
        sq0 = sb("sq0", [P, VK, D], F32, setup)
        nn0 = sb("nn0", [P, VK, 2, D], F32, setup)
        wk_s = sb("wk_s", [D, 4, P], F32, setup)
        wqt_s = sb("wqt_s", [P, 4, P], F32, setup)
        wvt_s = sb("wvt_s", [P, 4, D], F32, setup)
        wo_s = sb("wo_s", [P, HEADS, D], F32, setup)
        WVO = sb("WVO", [D, HEADS, D], F32, setup)
        VOs = sb("VOs", [P, VK, HEADS * D], F32, setup)
        VOr = sb("VOr", [P, NG, D], F32, setup)
        kT = sb("kT", [P, 4, NV], F32, setup)
        TS = sb("TS", [P, NG, 2, CG, HEADS], F32R, setup)
        OHt = sb("OHt", [P, 2, OB, NV], BF16, setup)
        As = [sb(f"As{i}", [P, 4, NV], F32, setup) for i in range(2)]
        setup.close()
        G2 = [sb(f"G2{i}", [P, FB, NV], F32, att) for i in range(G2_RING)]
        att.close()

        xb = [sb(f"xb{i}", [P, TOK], I32) for i in range(2)]
        OH = [sb(f"OH{i}", [P, VK, TOK], BF16) for i in range(2)]
        r1 = sb("r1", [P, VK, TB * D])
        r2 = [sb(f"r2{i}", [P, VK, TB * D], BF16) for i in range(2)]
        H2 = [sb(f"H2{i}", [P, TB, D]) for i in range(H_RING)]
        xc = sb("xc", [P, TB, D])
        sq = sb("sq", [P, TB, D])
        nrm = sb("nrm", [P, TB, D])
        NN = sb("NN", [P, TB, 2, D])
        st = sb("st", [P, 4, TB])
        X2 = [sb(f"X2{i}", [P, TOK], F32R) for i in range(RING)]
        RF = sb("RF", [P, TOK])
        RH = sb("RH", [P, TOK], F32R)
        lg = sb("lg", [P, TB, E])
        cmp_ = sb("cmp", [P, TB, E, E])
        rank = sb("rank", [P, TB, E])
        m0, m1, sg = (sb(n, [P, TB, E]) for n in ("m0", "m1", "sg"))
        ex, ps_, g0, g1 = (sb(n, [P, TB, E]) for n in ("ex", "ps_", "g0", "g1"))
        gate = sb("gate", [P, TB, E])
        rt = sb("rt", [P, 8, TB])
        GT = [sb(f"GT{i}", [TB * E, P]) for i in range(2)]
        WB = [sb(f"WB{i}", [P, PAIRS, TOK]) for i in range(RING)]
        GG = [sb(f"GG{i}", [D, HT]) for i in range(RING)]
        GP = sb("GP", [D, HT], F32R)
        H1 = [sb(f"H1{q}", [P, TOK]) for q in range(PAIRS)]
        H2g = [sb(f"H2g{q}", [P, TOK]) for q in range(PAIRS)]
        OT = sb("OT", [P, HT])
        Y = [sb(f"Y{i}", [P, TB, D]) for i in range(2)]

        ld_tab, ld_c, ld_x, ld_k, ld_q, ld_v, ld_o = (sem(n) for n in (
            "ld_tab", "ld_c", "ld_x", "ld_k", "ld_q", "ld_v", "ld_o"))
        ld_r, ld_w1, ld_b, ld_w2, ld_w3 = (sem(n) for n in ("ld_r", "ld_w1", "ld_b", "ld_w2", "ld_w3"))
        ln0, ln0_pool, const_ready, nT_ps, nT_sb, nd_hi, nd_lo, x_f, w_hi = (sem(n) for n in (
            "ln0", "ln0_pool", "const_ready", "nT_ps", "nT_sb", "nd_hi", "nd_lo", "x_f", "w_hi"))
        k_ps, k_sb, t_ps, t_hi, t_lo, t_dup = (sem(n) for n in ("k_ps", "k_sb", "t_ps", "t_hi", "t_lo", "t_dup"))
        wvo_ps, wvo_sb, vo_ps, vo_sb, vo_st, vo_ld, vo_hi, vo_ready = (sem(n) for n in (
            "wvo_ps", "wvo_sb", "vo_ps", "vo_sb", "vo_st", "vo_ld", "vo_hi", "vo_ready"))
        oh_ready, cnt_ps, cnt_sb = sem("oh_ready"), sem("cnt_ps"), sem("cnt_sb")
        lg_ps, as_ready, ah_hi, ah_dve, ah_pool = (sem(n) for n in ("lg_ps", "as_ready", "ah_hi", "ah_dve", "ah_pool"))
        ah_hi_act = sem("ah_hi_act")
        w_lo, bias_ps, sel_dve, bias_dve, w2_zero = (sem(n) for n in (
            "w_lo", "bias_ps", "sel_dve", "bias_dve", "w2_zero"))
        bd_dve, bd_act, g_ps, gs_act, gs_dve = (sem(n) for n in ("bd_dve", "bd_act", "g_ps", "gs_act", "gs_dve"))
        sent_sp = [sem(f"sent_sp{i}") for i in range(GS_RING)]
        sent_pool = [sem(f"sent_pool{i}") for i in range(GS_RING)]
        o_ps, o_sb, ot_ps, h_tab = (sem(n) for n in ("o_ps", "o_sb", "ot_ps", "h_tab"))
        x_ld = [sem(f"x_ld{i}") for i in range(2)]
        oh_b, r1_ok, r2_ok, h_ps, h_sb = (sem(n) for n in ("oh_b", "r1_ok", "r2_ok", "h_ps", "h_sb"))
        ln_dve, ln_act, ln_pool, nn_hi, nn_ready = (sem(n) for n in ("ln_dve", "ln_act", "ln_pool", "nn_hi", "nn_ready"))
        x_ps, x_sb, rh_ps, rf_sb, rh_hi, rh_ready = (sem(n) for n in ("x_ps", "x_sb", "rh_ps", "rf_sb", "rh_hi", "rh_ready"))
        rl_ps, rt_dve, ex_act, gate_ready, gt_ps, gt_sb = (sem(n) for n in (
            "rl_ps", "rt_dve", "ex_act", "gate_ready", "gt_ps", "gt_sb"))
        gate_st = [sem(f"gate_st{i}") for i in range(2)]
        wb_ld = [sem(f"wb_ld{i}") for i in range(RING)]
        gg_ld = [sem(f"gg_ld{i}") for i in range(RING)]
        gg_zero, gp_hi, gp_ready = sem("gg_zero"), sem("gp_hi"), sem("gp_ready")
        l1_ps, h1_sb, l2_ps, h2_sb, l3_ps, ot_sb, y_ps, y_sb = (sem(n) for n in (
            "l1_ps", "h1_sb", "l2_ps", "h2_sb", "l3_ps", "ot_sb", "y_ps", "y_sb"))
        y_st = [sem(f"y_st{i}") for i in range(2)]
        cmp_zero = sem("cmp_zero")

        B_G, B_O, B_OT = 0, 4, 6
        B_H, B_X, B_L1, B_L2, B_Y = 0, 1, 3, 5, 7

        def x_load(eng, i):
            eng.dma_start(xb[i % 2][:], x_flat[:, i * TOK:(i + 1) * TOK].broadcast_to([P, TOK]))\
               .then_inc(x_ld[i % 2], 16)

        def send_unit(eng, n, mine, done):
            half = n // 2
            eng.wait_ge(gs_act, 2 * n + 2)
            eng.wait_ge(gs_dve, 2 * n + 2)
            if n == 0:
                eng.wait_ge(ah_dve, 4)
                eng.wait_ge(ah_pool, 4)
                eng.wait_ge(cnt_sb, 1)
                eng.wait_ge(vo_ready, 1)
            if half >= G2_RING and n % 2 == 0:
                eng.wait_ge(o_ps, 4 * ((half - G2_RING) // 2 + 1))
            for m in mine:
                row = (n % 2) * UG + m
                eng.dma_start(G2[half % G2_RING][row * CG:(row + 1) * CG, :, :],
                              Gs[n % GS_RING][:, m, :]).then_inc(done[n % GS_RING], 16)

        def unit_sent(eng, n):
            eng.wait_ge(sent_sp[n % GS_RING], 16 * SP_DMAS * (n // GS_RING + 1))
            eng.wait_ge(sent_pool[n % GS_RING], 16 * POOL_DMAS * (n // GS_RING + 1))

        def table_of(i):
            return Htab[:, :, i * TB:(i + 1) * TB, :].rearrange("p k b f -> p k (b f)")

        def upper(ap):
            return ap.bitcast(BF16).rearrange("p k (n two) -> p k n two", two=2)[:, :, :, 1]

        def two_banks(b):
            return PS[:, b:b + 2, :].rearrange("p b n -> p (b n)")

        def l2_bank(q):
            return B_X if q == 2 else B_L2

        def vo_slice(n):
            fg, r = divmod(n, UPF)
            return VOp[:, :, r * UG:(r + 1) * UG, fg * FB:(fg + 1) * FB].bitcast(F32)

        def one_hots_with(t):
            return range(OH_EARLY + 2 * t, min(OH_EARLY + 2 * t + 2, NB // OB))

        def contraction_after(n):
            fg, r = divmod(n, UPF)
            if fg == 0 or r == 0:
                return ()
            m = 4 * (fg - 1) + r - 1
            return (m,) if r < 3 else (m, m + 1)

        def over(ap, n):
            return ap.unsqueeze(2).broadcast_to([ap.shape[0], ap.shape[1], n])

        def head_pair(ap, b):
            h = HEAD_ORDER[2 * b]
            return ap[:, :, :, h:h + 3:2].rearrange("p g c h -> p h g c")

        block = ctx.enter_context(nc.Block())

        @block.sync
        def _(sp):
            sp.dma_start(table[:], tab.rearrange("(k p) d -> p k d", p=P)).then_inc(ld_tab, 16)
            sp.dma_start(cst[:], consts).then_inc(ld_c, 16)
            sp.dma_start(wk_s[:], wk.rearrange("d (q m) -> d q m", m=P)).then_inc(ld_k, 16)
            sp.dma_start(wqt_s[:], wqt.rearrange("(q p) d -> p q d", p=P)).then_inc(ld_q, 16)
            sp.dma_start(r1_raw[:], rw1).then_inc(ld_r, 16)
            sp.dma_start(r2_raw[:], rw2).then_inc(ld_r, 16)
            sp.dma_start(rb1_s[:], rb1).then_inc(ld_r, 16)
            sp.dma_start(rb2_s[:], rb2.broadcast_to([P, E])).then_inc(ld_r, 16)
            sp.dma_start(w1_raw[:], w1).then_inc(ld_w1, 16)
            sp.wait_ge(vo_sb, VK)
            sp.dma_start(vo_dram.rearrange("(k p) h f -> p k (h f)", p=P), VOs[:]).then_inc(vo_st, 16)
            sp.wait_ge(vo_st, 16)
            for u in range(2):
                sp.dma_start(VOr[u * D:(u + 1) * D, :, :],
                             vo_dram.rearrange("(g c) h f -> (c h) g f", c=CG)).then_inc(vo_ld, 16)
            for n in range(UNITS):
                send_unit(sp, n, range(SP_DMAS), sent_sp)
            sp.wait_ge(o_ps, NF * 4)
            sp.wait_ge(h_tab, NF * 4 * VK)
            x_load(sp, 0)
            x_load(sp, 1)
            sp.wait_ge(oh_b, VK)
            x_load(sp, 2)
            for i in range(STEPS + LAG):
                if i < STEPS:
                    if i + 3 < STEPS:
                        sp.wait_ge(oh_b, VK * (i + 2))
                        x_load(sp, i + 3)
                    sp.wait_ge(gt_sb, i + 1)
                    if i >= RING:
                        sp.wait_ge(wb_ld[i % RING], 32 * (i // RING))
                        sp.wait_ge(gg_ld[i % RING], 128 * (i // RING))
                    sp.dma_start(gate_dram[i % RING].rearrange("e (t k) -> t e k", k=S),
                                 GT[i % 2][:]).then_inc(gate_st[i % 2], 16)
                    sp.wait_ge(gate_st[i % 2], 16 * (i // 2 + 1))
                    if i >= RING:
                        sp.wait_ge(h2_sb, PAIRS * (i - RING + 1))
                        sp.wait_ge(gp_ready, i - RING + 1)
                    for e in range(2):
                        src = gate_dram[i % RING].rearrange("(q e) k -> e q k", e=2)[e:e + 1]
                        sp.dma_start(WB[i % RING][e * D:(e + 1) * D, :, :],
                                     src.broadcast_to([D, PAIRS, TOK])).then_inc(wb_ld[i % RING], 16)
                    if i == 0:
                        sp.wait_ge(gg_zero, RING)
                    for w in range(2):
                        for u in range(2):
                            for z in range(2):
                                sp.dma_start(
                                    GG[i % RING][32 * w + 12 * u + 6 * z:32 * w + 12 * u + 6 * z + 6, :],
                                    gate_dram[i % RING][:, u * HT:(u + 1) * HT],
                                ).then_inc(gg_ld[i % RING], 16)
                if i >= LAG:
                    s = i - LAG
                    sp.wait_ge(y_sb, s + 1)
                    sp.dma_start(out[s * TB:(s + 1) * TB].rearrange("t p f -> p t f"),
                                 Y[s % 2][:]).then_inc(y_st[s % 2], 16)
            for i in range(2):
                sp.wait_ge(y_st[i], 16 * (STEPS // 2))

        @block.gpsimd
        def _(pool):
            pool.memset(mhalf[:], -0.5).then_inc(const_ready, 1)
            pool.memset(ones_b[:], 1.0).then_inc(const_ready, 1)
            pool.memset(W2s[:], 0.0).then_inc(w2_zero, 1)
            pool.wait_ge(w2_zero, 1)
            for e in range(2):
                pool.dma_start(W2s[e * D:(e + 1) * D, :, e * D:(e + 1) * D],
                               w2.rearrange("(q e) h f -> e h q f", e=2)[e]).then_inc(ld_w2, 16)
            pool.wait_ge(ln0, 4)
            pool.tensor_scalar(lnt[:, 2, :], lnt[:, 1, :], 1.0 / D, EPS, ALU.mult, ALU.add).then_inc(ln0_pool, 1)
            pool.wait_ge(ln0_pool, 1)
            pool.wait_ge(const_ready, 2)
            pool.tensor_tensor(lnt[:, 3, :], lnt[:, 2, :], mhalf[:, 0:VK], ALU.pow).then_inc(ln0_pool, 1)
            for t in range(1, 8, 2):
                pool.wait_ge(ah_hi_act, t // 2 + 1)
                rows = slice(4 * t, 4 * t + 4)
                pool.tensor_tensor(AH[D:P, rows, :], As[t % 2][D:P], AH[D:P, rows, :].bitcast(F32),
                                   ALU.subtract).then_inc(ah_pool, 1)
            for n in range(UNITS):
                send_unit(pool, n, range(SP_DMAS, UG), sent_pool)

            pool.wait_ge(o_ps, NF * 4)
            pool.wait_ge(h_tab, NF * 4 * VK)
            for i in range(RING):
                pool.memset(GG[i][:], 0.0).then_inc(gg_zero, 1)
            pool.memset(cmp_[:], 0.0).then_inc(cmp_zero, 1)

            def cut(i):
                h = table_of(i)
                pool.wait_ge(nn_ready, i - 1)
                if i - 3 >= LAG:
                    pool.wait_ge(gp_ready, i - 2 - LAG)
                pool.wait_ge(h_ps, i)
                pool.wait_ge(r2_ok, i)
                pool.tensor_tensor(r1[:], h, upper(h), ALU.subtract).then_inc(r1_ok, 1)
                pool.wait_ge(r1_ok, i + 1)
                pool.tensor_tensor(r2[i % 2][:], r1[:], upper(r1[:]), ALU.subtract).then_inc(r2_ok, 1)

            def normalise(i):
                pool.wait_ge(ln_dve, 4 * i + 3)
                if i >= 1:
                    pool.wait_ge(r2_ok, min(i + 2, STEPS))
                pool.tensor_scalar(st[:, 2, :], st[:, 1, :], 1.0 / D, EPS, ALU.mult, ALU.add).then_inc(ln_pool, 1)
                pool.wait_ge(ln_pool, 2 * i + 1)
                pool.tensor_tensor(st[:, 3, :], st[:, 2, :], mhalf[:], ALU.pow).then_inc(ln_pool, 1)
                pool.wait_ge(nn_hi, i + 1)
                pool.tensor_tensor(NN[:, :, 1, :], nrm[:], NN[:, :, 0, :], ALU.subtract).then_inc(nn_ready, 1)

            normalise(0)
            for i in range(STEPS + LAG):
                s = i - LAG
                if i + 1 < STEPS:
                    normalise(i + 1)
                if s >= 0:
                    pool.wait_ge(gp_hi, s + 1)
                    if i + 1 < STEPS:
                        pool.wait_ge(nn_ready, i + 2)
                    elif s >= 1:
                        pool.wait_ge(gp_ready, s)
                    pool.tensor_tensor(GP[32:D], GG[s % RING][32:D], GP[32:D].bitcast(F32), ALU.subtract)\
                        .then_inc(gp_ready, 1)
                if i + 3 < STEPS:
                    cut(i + 3)

        @block.scalar
        def _(act):
            act.dma_start(xt_i[:], x_t).then_inc(ld_x, 16)
            act.dma_start(wvt_s[:], wvt.rearrange("(q p) d -> p q d", p=P)).then_inc(ld_v, 16)
            act.dma_start(wo_s[:], wo.rearrange("p (h o) -> p h o", o=D)).then_inc(ld_o, 16)
            act.dma_start(b1_s[:], b1).then_inc(ld_b, 16)
            act.dma_start(b2_s[:], b2).then_inc(ld_b, 16)
            act.dma_start(b3_s[:], b3).then_inc(ld_b, 16)
            act.dma_start(W3s[:], w3.rearrange("(q p) o -> p q o", p=P)).then_inc(ld_w3, 16)
            act.wait_ge(wvo_ps, 1)
            for odd in range(2):
                act.activation(WVO[:, odd::2, :], PS[0:D, 5 + 2 * odd, 0:4 * D].rearrange("p (h o) -> p h o", o=D),
                               ACT.Copy).then_inc(wvo_sb, 1)
            act.wait_ge(nT_ps, 1)
            act.activation(nT[:], PS[:, 6, 0:NV], ACT.Copy).then_inc(nT_sb, 1)
            for b in range(2):
                act.wait_ge(k_ps, b + 1)
                act.activation(kT[:, 2 * b:2 * b + 2, :].rearrange("p q c -> p (q c)"), PS[:, b, :], ACT.Copy)\
                   .then_inc(k_sb, 1)
            for k in range(VK):
                act.wait_ge(vo_ps, k + 1)
                act.activation(VOs[:, k, :], PS[:, 6 + k, :], ACT.Copy).then_inc(vo_sb, 1)
            for b in range(4):
                act.wait_ge(t_ps, b + 1)
                act.activation(head_pair(TS[:, :, 0], b),
                               PS[:, T_BANKS[b], :].rearrange("p (h g c) -> p h g c", h=2, c=CG), ACT.Copy)\
                   .then_inc(t_hi, 1)
            for t in range(8):
                act.wait_ge(lg_ps, t + 1)
                if t >= 2:
                    if t % 2 == 0:
                        act.wait_ge(ah_dve, t // 2)
                    else:
                        act.wait_ge(ah_pool, t // 2)
                b = 2 * (t % 2)
                act.activation(As[t % 2][:].rearrange("p g a -> p (g a)"),
                               PS[:, b:b + 2, :].rearrange("p b n -> p (b n)"), ACT.Sigmoid, scale=SCALE)\
                   .then_inc(as_ready, 1)
                if t % 2:
                    act.wait_ge(as_ready, t + 1)
                    act.activation(AH[:, 4 * t:4 * t + 4, :], As[1][:], ACT.Copy).then_inc(ah_hi_act, 1)

            def bd(n):
                if n == 0:
                    act.wait_ge(vo_ready, 1)
                if n >= BD_RING:
                    act.wait_ge(g_ps, 4 * (n - BD_RING + 1))
                for c in range(BD_DVE, CG):
                    ins = act.activation(BD[n % BD_RING][:, :, :, c, :], vo_slice(n), ACT.Copy,
                                         scale=cst[:, C_MASK + c:C_MASK + c + 1])
                ins.then_inc(bd_act, 1)

            def o_evac(m):
                act.wait_ge(o_ps, m + 1)
                if m >= 2:
                    act.wait_ge(ot_ps, m - 1)
                act.activation(O1[m % 2][:], PS[:, B_O + m % 2, :], ACT.Copy).then_inc(o_sb, 1)

            bd(0)
            bd(1)
            for n in range(UNITS):
                if n >= GS_RING:
                    unit_sent(act, n - GS_RING)
                for j in (0, 2):
                    act.wait_ge(g_ps, 4 * n + j + 1)
                    act.activation(Gs[n % GS_RING][:, 2 * j:2 * j + 2, :].rearrange("p g a -> p (g a)"),
                                   PS[:, B_G + j, :], ACT.Copy).then_inc(gs_act, 1)
                if n + 2 < UNITS:
                    bd(n + 2)
                for m in contraction_after(n):
                    o_evac(m)
            for m in range(4 * (NF - 1), 4 * NF):
                o_evac(m)

            def relu1(s, q):
                act.wait_ge(l1_ps, PAIRS * s + q + 1)
                if s >= 1:
                    act.wait_ge(l2_ps, PAIRS * (s - 1) + q + 1)
                act.activation(H1[q][:], two_banks(B_L1), ACT.Relu, bias=b1_s[:, q:q + 1]).then_inc(h1_sb, 1)

            def take_h(i):
                act.wait_ge(h_ps, i + 1)
                if i >= H_RING:
                    act.wait_ge(y_sb, i - H_RING + 1)
                act.activation(H2[i % H_RING][:].rearrange("p t f -> p (t f)"), PS[:, B_H, :], ACT.Copy)\
                   .then_inc(h_sb, 1)

            def gates_hi(s):
                act.wait_ge(gg_ld[s % RING], 128 * (s // RING + 1))
                if s >= 1:
                    act.wait_ge(l3_ps, s)
                act.activation(GP[:], GG[s % RING][:], ACT.Copy).then_inc(gp_hi, 1)

            def squares(i):
                act.wait_ge(ln_dve, 4 * i + 2)
                act.activation(sq[:], xc[:], ACT.Square).then_inc(ln_act, 1)

            def rows_hi(i):
                act.wait_ge(ln_dve, 4 * i + 4)
                if i >= 1:
                    act.wait_ge(nn_ready, i)
                    act.wait_ge(x_ps, 2 * i)
                act.activation(NN[:, :, 0, :].bitcast(F32R), nrm[:], ACT.Copy).then_inc(nn_hi, 1)

            def rows_out(i):
                act.wait_ge(x_ps, 2 * i + 2)
                if i >= RING:
                    act.wait_ge(l1_ps, PAIRS * (i - RING + 1))
                act.activation(X2[i % RING][:], two_banks(B_X), ACT.Copy).then_inc(x_sb, 1)

            act.wait_ge(ld_b, 48)
            act.wait_ge(ld_r, 64)
            take_h(0)
            squares(0)
            rows_hi(0)
            take_h(1)
            rows_out(0)
            for i in range(STEPS + LAG):
                a, b, s, ahead = i < STEPS, i >= LAG, i - LAG, i + 1 < STEPS
                if ahead:
                    squares(i + 1)
                if a:
                    act.wait_ge(rh_ps, i + 1)
                    if i >= 1:
                        act.wait_ge(rh_ready, i)
                    act.activation(RF[:], two_banks(B_X), ACT.Relu, bias=rb1_s[:, 0:1]).then_inc(rf_sb, 1)
                    act.wait_ge(rf_sb, i + 1)
                    if i >= 1:
                        act.wait_ge(rl_ps, i)
                    act.activation(RH[:], RF[:], ACT.Copy).then_inc(rh_hi, 1)
                if b:
                    relu1(s, 1)
                    gates_hi(s)
                if a:
                    act.wait_ge(rt_dve, RT * i + 3)
                    act.activation(ex[:], ex[:], ACT.Exp).then_inc(ex_act, 1)
                if b:
                    relu1(s, 2)
                if ahead:
                    rows_hi(i + 1)
                if a:
                    act.wait_ge(rt_dve, RT * i + 13)
                    act.activation(rt[:, 4, :], rt[:, 3, :], ACT.Exp, scale=-1.0).then_inc(ex_act, 1)
                if 0 <= s + 1 < STEPS:
                    relu1(s + 1, 0)
                if i + 2 < STEPS:
                    take_h(i + 2)
                if ahead:
                    rows_out(i + 1)
                if b:
                    act.wait_ge(l3_ps, s + 1)
                    act.activation(OT[:], PS[:, B_Y, :], ACT.Copy).then_inc(ot_sb, 1)
                if a:
                    act.wait_ge(gt_ps, i + 1)
                    if i >= 2:
                        act.wait_ge(gate_st[i % 2], 16 * (i // 2))
                    act.activation(GT[i % 2][:], PS[0:TB * E, B_L2, 0:P], ACT.Copy).then_inc(gt_sb, 1)

        @block.tensor
        def _(pe):
            pe.wait_ge(ld_v, 16)
            pe.wait_ge(ld_o, 16)
            for h in HEAD_ORDER:
                rows = slice(D * (h % 2), D * (h % 2) + D)
                ins = pe.matmul(PS[0:D, 5 + 2 * (h % 2), h // 2 * D:(h // 2 + 1) * D], wvt_s[rows, h // 2, :],
                                wo_s[rows, h, :], start=True, stop=True)
            ins.then_inc(wvo_ps, 1)
            pe.wait_ge(const_ready, 2)
            pe.wait_ge(wvo_sb, 2)

            def count(a):
                pe.wait_ge(oh_ready, a + 1)
                for b in range(OB):
                    for k in range(VK):
                        c = k * NB + a * OB + b
                        ins = pe.matmul(PS[:, 5, c:c + 1], OHt[:, a % 2, b, k * P:(k + 1) * P],
                                        ones_b[:, 0:1], start=True, stop=True)
                ins.then_inc(cnt_ps, 1)

            count(0)
            count(1)
            pe.wait_ge(ld_c, 16)
            pe.wait_ge(ln0, 6)
            for k in range(VK):
                ins = pe.transpose(PS[:, 6, k * P:(k + 1) * P], nn0[:, k].rearrange("p u d -> p (u d)"), ident)
            ins.then_inc(nT_ps, 1)
            pe.wait_ge(ld_k, 16)
            pe.wait_ge(nT_sb, 1)
            for q in range(4):
                ins = pe.matmul(PS[:, q // 2, (q % 2) * NV:(q % 2 + 1) * NV], wk_s[:, q, :], nT[0:D, :],
                                start=True, stop=True)
                if q % 2:
                    ins.then_inc(k_ps, 1)
                    count(2 + q // 2)
            for k in range(VK):
                pe.matmul(PS[:, 6 + k, :], nT[0:D, k * P:(k + 1) * P],
                          WVO[:].rearrange("d h o -> d (h o)"), start=True, stop=True)\
                  .then_inc(vo_ps, 1)
                count(4 + k)
            pe.wait_ge(ld_q, 16)
            pe.wait_ge(k_sb, 2)
            for x, h in enumerate(HEAD_ORDER):
                rows = slice(D * (h % 2), D * (h % 2) + D)
                ins = pe.matmul(PS[:, T_BANKS[x // 2], (x % 2) * NV:(x % 2 + 1) * NV], wqt_s[rows, h // 2, :],
                                kT[rows, h // 2, :], start=True, stop=True)
                if x % 2:
                    ins.then_inc(t_ps, 1)
            for a in range(OH_EARLY - 2, OH_EARLY):
                count(a)
            pe.wait_ge(sel_dve, 1)
            pe.wait_ge(ld_w3, 16)
            pe.wait_ge(vo_sb, 1)
            for q in range(PAIRS):
                ins = pe.matmul(PS[0:D, 6, 0:D], selb2[:, q, :], W3s[:, q, :], start=(q == 0), stop=(q == 2))
            ins.then_inc(bias_ps, 1)
            pe.wait_ge(nd_lo, 1)
            pe.wait_ge(t_dup, 2)
            for t in range(8):
                if t >= 2:
                    pe.wait_ge(as_ready, t - 1)
                for j in range(4):
                    o = PS[:, 2 * (t % 2) + j // 2, (j % 2) * NV:(j % 2 + 1) * NV]
                    w = TS[:, 4 * t + j].rearrange("p u c h -> p (u c h)")
                    pe.matmul(o, w, NDhi[:], start=True, stop=False)
                    ins = pe.matmul(o, w, NDlo[:], start=False, stop=True)
                ins.then_inc(lg_ps, 1)
                if t >= 2:
                    for a in one_hots_with(t - 2):
                        count(a)

            def unit(n):
                pe.wait_ge(bd_dve, n + 1)
                pe.wait_ge(bd_act, n + 1)
                r = n % UPF
                for j in range(4):
                    if n == 0 and j == 0:
                        pe.wait_ge(as_ready, 8)
                    if r < 4 and n < UPF and j % 2 == 0:
                        t = 2 * r + j // 2
                        pe.wait_ge(ah_pool if t % 2 else ah_dve, t // 2 + 1)
                    if n >= 1:
                        pe.wait_ge(gs_dve if j % 2 else gs_act, 2 * (n - 1) + j // 2 + 1)
                    for m in range(2):
                        gl = 2 * j + m
                        o = PS[:, B_G + j, m * NV:(m + 1) * NV]
                        for part in range(2):
                            ins = pe.matmul(o, BD[n % BD_RING][:, part, gl].rearrange("p c f -> p (c f)"),
                                            AH[:, r * UG + gl, :], start=(part == 0), stop=(part == 1))
                    ins.then_inc(g_ps, 1)

            def contract(m):
                fg, j = divmod(m, 4)
                if m == 0:
                    pe.wait_ge(cnt_sb, 1)
                    pe.wait_ge(bias_dve, 1)
                if j == 0:
                    for n in range(UPF * fg, UPF * (fg + 1)):
                        unit_sent(pe, n)
                if m >= 2:
                    pe.wait_ge(o_sb, m - 1)
                for k in range(VK):
                    for u in range(2):
                        f = (FB // 2) * u + 2 * j
                        ins = pe.matmul(PS[u * NB:(u + 1) * NB, B_O + m % 2, :], cnt[:, k, :],
                                        G2[(2 * fg + k) % G2_RING][:, f:f + 2, :].rearrange("p f a -> p (f a)"),
                                        start=(k == 0), stop=(k == 1), skip_group_check=True)
                ins.then_inc(o_ps, 1)

            def turn(m):
                pe.wait_ge(o_sb, m + 1)
                if m >= 2:
                    pe.wait_ge(h_tab, VK * (m - 1))
                for x in range(4):
                    ins = pe.transpose(PS[:, B_OT + m % 2, x * P:(x + 1) * P], O1[m % 2][:, x * P:(x + 1) * P], ident)
                ins.then_inc(ot_ps, 1)

            for n in range(UNITS):
                unit(n)
                for m in contraction_after(n):
                    contract(m)
                    if m >= 1:
                        turn(m - 1)
            for m in range(4 * (NF - 1), 4 * NF):
                contract(m)
                turn(m - 1)
            turn(4 * NF - 1)

            def gather(i):
                pe.wait_ge(oh_b, VK * (i + 1))
                pe.wait_ge(r2_ok, i + 1)
                if i == 0:
                    pe.wait_ge(h_tab, NF * 4 * VK)
                if i >= 1:
                    pe.wait_ge(h_sb, i)
                parts = (upper(table_of(i)), upper(r1[:]), r2[i % 2][:])
                for t in range(TB):
                    for k in range(VK):
                        for x, part in enumerate(parts):
                            ins = pe.matmul(PS[:, B_H, t * D:(t + 1) * D], OH[i % 2][:, k, t * S:(t + 1) * S],
                                            part[:, k, t * D:(t + 1) * D], start=(k == 0 and x == 0),
                                            stop=(k == 1 and x == 2))
                ins.then_inc(h_ps, 1)

            def turn_rows(i):
                pe.wait_ge(nn_hi, i + 1)
                if i > LAG:
                    pe.wait_ge(h2_sb, PAIRS * (i - LAG))
                pe.wait_ge(nn_ready, i + 1)
                if i >= 1:
                    pe.wait_ge(rf_sb, i)
                for t in range(TB):
                    ins = pe.transpose(PS[:, B_X + t // 4, (t % 4) * P:(t % 4 + 1) * P],
                                       NN[:, t].rearrange("p u d -> p (u d)"), ident)
                    if t % 4 == 3:
                        ins.then_inc(x_ps, 1)

            def hidden(i):
                pe.wait_ge(x_sb, i + 1)
                if i == 0:
                    pe.wait_ge(w_lo, 4)
                for part, w in enumerate((R1hi, R1lo)):
                    for u in range(2):
                        ins = pe.matmul(PS[:, B_X + u, :], w[:], X2[i % RING][:, u * HT:(u + 1) * HT],
                                        start=(part == 0), stop=(part == 1), skip_group_check=True)
                ins.then_inc(rh_ps, 1)

            def router(i):
                pe.wait_ge(rh_ready, i + 1)
                if i > LAG:
                    pe.wait_ge(y_sb, i - LAG)
                elif i >= 1:
                    pe.wait_ge(rt_dve, RT * (i - 1) + 1)
                for t in range(TB):
                    ins = pe.matmul(PS[:, B_Y, t * E:(t + 1) * E], RH[:, t * P:(t + 1) * P], R2[:],
                                    start=True, stop=True)
                ins.then_inc(rl_ps, 1)

            def turn_gates(i):
                pe.wait_ge(gate_ready, i + 1)
                if i >= 1:
                    pe.wait_ge(gt_sb, i)
                if i >= LAG:
                    pe.wait_ge(h2_sb, PAIRS * (i - LAG + 1))
                pe.transpose(PS[0:TB * E, B_L2, 0:P], gate[:].rearrange("p t e -> p (t e)"), ident)\
                  .then_inc(gt_ps, 1)

            def layer1(s, q):
                if PAIRS * s + q >= 1:
                    pe.wait_ge(h1_sb, PAIRS * s + q)
                for part, w in enumerate((W1hi, W1lo)):
                    for u in range(2):
                        ins = pe.matmul(PS[:, B_L1 + u, :], w[:, q * P:(q + 1) * P],
                                        X2[s % RING][:, u * HT:(u + 1) * HT], start=(part == 0), stop=(part == 1),
                                        skip_group_check=True)
                ins.then_inc(l1_ps, 1)

            def layer2(s, q):
                pe.wait_ge(h1_sb, PAIRS * s + q + 1)
                if s == 0 and q == 0:
                    pe.wait_ge(ld_w2, 32)
                if q == 0:
                    pe.wait_ge(gt_sb, min(s + LAG, STEPS))
                if q == 2:
                    pe.wait_ge(rf_sb, min(s + LAG + 1, STEPS))
                elif PAIRS * s + q >= 1:
                    pe.wait_ge(h2_sb, PAIRS * s + q)
                for u in range(2):
                    ins = pe.matmul(PS[:, l2_bank(q) + u, :], W2s[:, q, :], H1[q][:, u * HT:(u + 1) * HT],
                                    start=True, stop=True)
                ins.then_inc(l2_ps, 1)

            def layer3(s, q):
                pe.wait_ge(h2_sb, PAIRS * s + q + 1)
                if q == 0:
                    if s >= 1:
                        pe.wait_ge(y_sb, s)
                    if s + LAG < STEPS:
                        pe.wait_ge(rt_dve, RT * (s + LAG) + 1)
                for u in range(2):
                    ins = pe.matmul(PS[u * D:(u + 1) * D, B_Y, :], W3s[:, q, :], H2g[q][:, u * HT:(u + 1) * HT],
                                    start=(q == 0), stop=False, skip_group_check=True)
                if q == PAIRS - 1:
                    pe.wait_ge(gp_ready, s + 1)
                    ins = pe.matmul(PS[:, B_Y, :], BB[:].rearrange("p u o -> p (u o)"), GP[:], start=False, stop=True,
                                    skip_group_check=True)
                    ins.then_inc(l3_ps, 1)

            def turn_out(s):
                pe.wait_ge(ot_sb, s + 1)
                for j in range(4):
                    ins = pe.transpose(PS[:, B_Y, j * P:(j + 1) * P], OT[:, j * P:(j + 1) * P], ident)
                ins.then_inc(y_ps, 1)

            gather(0)
            gather(1)
            turn_rows(0)
            hidden(0)
            for i in range(STEPS + LAG):
                a, b, s, ahead = i < STEPS, i >= LAG, i - LAG, i + 1 < STEPS
                if b:
                    layer1(s, 1)
                    layer2(s, 0)
                if i + 2 < STEPS:
                    gather(i + 2)
                if a:
                    router(i)
                if b:
                    layer1(s, 2)
                    layer2(s, 1)
                    layer3(s, 0)
                    layer2(s, 2)
                if 0 <= s + 1 < STEPS:
                    layer1(s + 1, 0)
                if b:
                    layer3(s, 1)
                if ahead:
                    turn_rows(i + 1)
                if b:
                    layer3(s, 2)
                if a:
                    turn_gates(i)
                if ahead:
                    hidden(i + 1)
                if b:
                    turn_out(s)

        @block.vector
        def _(dve):
            dve.wait_ge(ld_tab, 16)
            dve.tensor_reduce(lnt[:, 0, :], table[:], AX.X, ALU.add).then_inc(ln0, 1)
            dve.wait_ge(ln0, 1)
            dve.scalar_tensor_tensor(out=xc0[:], in0=lnt[:, 0, :].unsqueeze(2).broadcast_to([P, VK, D]),
                                     scalar=-1.0 / D, in1=table[:], op0=ALU.mult, op1=ALU.add).then_inc(ln0, 1)
            dve.wait_ge(ln0, 2)
            dve.tensor_tensor(sq0[:], xc0[:], xc0[:], ALU.mult).then_inc(ln0, 1)
            dve.wait_ge(ln0, 3)
            dve.tensor_reduce(lnt[:, 1, :], sq0[:], AX.X, ALU.add).then_inc(ln0, 1)
            dve.wait_ge(ld_c, 16)
            dve.wait_ge(ld_x, 16)
            dve.tensor_copy(iota_b[:], cst[:, C_ROW:C_ROW + NV]).then_inc(x_f, 1)
            dve.tensor_copy(xt_f[:], xt_i[:]).then_inc(x_f, 1)
            dve.wait_ge(x_f, 2)

            def one_hots(a):
                if a >= 2:
                    dve.wait_ge(cnt_ps, a - 1)
                for b in range(OB):
                    ins = dve.tensor_scalar(OHt[:, a % 2, b, :], iota_b[:], xt_f[:, OB * a + b:OB * a + b + 1],
                                            None, ALU.is_equal)
                ins.then_inc(oh_ready, 1)

            one_hots(0)
            one_hots(1)
            dve.wait_ge(ln0_pool, 2)
            for u in range(2):
                dve.tensor_tensor(nn0[:, :, u, :], xc0[:], lnt[:, 3, :].unsqueeze(2).broadcast_to([P, VK, D]),
                                  ALU.mult).then_inc(ln0, 1)
            dve.wait_ge(nT_sb, 1)
            dve.tensor_copy(NDhi[:], nT[:]).then_inc(nd_hi, 1)
            dve.wait_ge(nd_hi, 1)
            dve.tensor_tensor(NDlo[:], nT[:], NDhi[:].bitcast(F32), ALU.subtract).then_inc(nd_lo, 1)
            for a in range(2, OH_EARLY):
                one_hots(a)
            dve.wait_ge(ld_b, 48)
            for q in range(PAIRS):
                ins = dve.tensor_scalar(selb2[:, q, :], cst[:, C_SEL + q * D:C_SEL + (q + 1) * D], b2_s[:, q:q + 1],
                                        None, ALU.mult)
            ins.then_inc(sel_dve, 1)
            dve.tensor_scalar(nb2_s[:], b2_s[:], -1.0, None, ALU.mult).then_inc(sel_dve, 1)
            for b in range(4):
                dve.wait_ge(t_hi, b + 1)
                v = head_pair(TS[D:P, :, 0], b)
                dve.tensor_tensor(v, PS[D:P, T_BANKS[b], :].rearrange("p (h g c) -> p h g c", h=2, c=CG),
                                  v.bitcast(F32), ALU.subtract).then_inc(t_lo, 1)
            dve.wait_ge(t_lo, 4)
            for x in range(2):
                g = slice(x * NG // 2, (x + 1) * NG // 2)
                dve.tensor_copy(TS[:, g, 1], TS[:, g, 0].bitcast(F32)).then_inc(t_dup, 1)
            for t in range(8):
                if t % 2 == 0:
                    rows = slice(4 * t, 4 * t + 4)
                    dve.wait_ge(as_ready, t + 1)
                    dve.tensor_copy(AH[:, rows, :], As[0][:]).then_inc(ah_hi, 1)
                    dve.wait_ge(ah_hi, t // 2 + 1)
                    dve.tensor_tensor(AH[D:P, rows, :], As[0][D:P], AH[D:P, rows, :].bitcast(F32),
                                      ALU.subtract).then_inc(ah_dve, 1)
                for a in one_hots_with(t):
                    one_hots(a)
                if t == VO_AT:
                    dve.wait_ge(vo_ld, 32)
                    dve.tensor_copy(VOp[:, 0], VOr[:]).then_inc(vo_hi, 1)
                if t == VO_AT + 1:
                    dve.wait_ge(vo_hi, 1)
                    dve.tensor_tensor(VOp[:, 1], VOr[:], VOp[:, 0].bitcast(F32), ALU.subtract).then_inc(vo_ready, 1)
            dve.wait_ge(cnt_ps, NB // OB)
            dve.tensor_copy(cnt[:].rearrange("p k b -> p (k b)"), PS[:, 5, 0:VK * NB]).then_inc(cnt_sb, 1)

            def bd(n):
                if n == 0:
                    dve.wait_ge(vo_ready, 1)
                if n >= BD_RING:
                    dve.wait_ge(g_ps, 4 * (n - BD_RING + 1))
                for c in range(BD_DVE):
                    ins = dve.tensor_scalar(BD[n % BD_RING][:, :, :, c, :], vo_slice(n),
                                            cst[:, C_MASK + c:C_MASK + c + 1], None, ALU.mult)
                ins.then_inc(bd_dve, 1)

            def table_rows(m):
                fg, j = divmod(m, 4)
                dve.wait_ge(ot_ps, m + 1)
                for k in range(VK):
                    f0 = fg * FB + 2 * j
                    o = Htab[:, k].rearrange("p b (f2 u f) -> p f2 u f b", u=2, f=FB // 2)[:, fg, :, 2 * j:2 * j + 2, :]
                    e = table[:, k].rearrange("p (f2 u f) -> p f2 u f", u=2, f=FB // 2)[:, fg, :, 2 * j:2 * j + 2]
                    for f in range(2):
                        src = PS[:, B_OT + m % 2, (2 * f + k) * P:(2 * f + k + 1) * P].rearrange(
                            "p (u b) -> p u b", u=2)
                        ins = dve.scalar_tensor_tensor(
                            out=o[:, :, f, :], in0=src, scalar=0.0,
                            in1=e[:, :, f].unsqueeze(2).broadcast_to([P, 2, NB]), op0=ALU.max, op1=ALU.add)
                    ins.then_inc(h_tab, 1)

            def mixture_weights(n):
                if n == 0:
                    dve.wait_ge(bias_ps, 1)
                    dve.tensor_tensor(b3f[:], PS[0:D, 6, 0:D], b3_s[:], ALU.add).then_inc(bias_dve, 1)
                    dve.wait_ge(bias_dve, 1)
                    dve.tensor_copy(b3hi[:], b3f[:]).then_inc(bias_dve, 1)
                    dve.wait_ge(ld_r, 64)
                    dve.tensor_copy(R1hi[:], r1_raw[:]).then_inc(w_hi, 1)
                    dve.tensor_copy(R2[:], r2_raw[:]).then_inc(w_hi, 1)
                    dve.wait_ge(ld_w1, 16)
                    dve.tensor_copy(W1hi[:], w1_raw[:]).then_inc(w_hi, 1)
                if n == 1:
                    dve.wait_ge(bias_dve, 2)
                    dve.tensor_tensor(b3lo[:], b3f[:], b3hi[:].bitcast(F32), ALU.subtract).then_inc(bias_dve, 1)
                    for u in range(2):
                        dve.tensor_scalar(b3t[:, u, :], b3hi[:].bitcast(F32), cst[0:D, C_BM + u:C_BM + u + 1], None,
                                          ALU.mult).then_inc(bias_dve, 1)
                    dve.wait_ge(w_hi, 3)
                    dve.tensor_tensor(R1lo[:], r1_raw[:], R1hi[:].bitcast(F32), ALU.subtract).then_inc(w_lo, 1)
                    for r in (32, 96):
                        dve.tensor_tensor(R2[r:r + 32], r2_raw[r:r + 32], R2[r:r + 32].bitcast(F32), ALU.subtract)\
                           .then_inc(w_lo, 1)
                    dve.tensor_tensor(W1lo[:], w1_raw[:], W1hi[:].bitcast(F32), ALU.subtract).then_inc(w_lo, 1)
                if n == 2:
                    dve.wait_ge(bias_dve, 5)
                    for u in range(2):
                        dve.scalar_tensor_tensor(out=BB[:, u, :], in0=b3lo[:],
                                                 scalar=cst[0:D, C_BM + 2 + u:C_BM + 3 + u], in1=b3t[:, u, :],
                                                 op0=ALU.mult, op1=ALU.add).then_inc(bias_dve, 1)

            bd(0)
            bd(1)
            for n in range(UNITS):
                if n >= GS_RING:
                    unit_sent(dve, n - GS_RING)
                for j in (1, 3):
                    dve.wait_ge(g_ps, 4 * n + j + 1)
                    dve.tensor_copy(Gs[n % GS_RING][:, 2 * j:2 * j + 2, :].rearrange("p g a -> p (g a)"),
                                    PS[:, B_G + j, :]).then_inc(gs_dve, 1)
                if n + 2 < UNITS:
                    bd(n + 2)
                mixture_weights(n)
                for m in contraction_after(n):
                    if m >= 1:
                        table_rows(m - 1)
            for m in range(4 * (NF - 1) - 1, 4 * NF):
                table_rows(m)

            def one_hot_ids(i):
                dve.wait_ge(x_ld[i % 2], 16 * (i // 2 + 1))
                if i >= 2:
                    dve.wait_ge(h_ps, i - 1)
                for k in range(VK):
                    dve.tensor_scalar(OH[i % 2][:, k, :], xb[i % 2][:], cst[:, C_IOTA + k:C_IOTA + k + 1], None,
                                      ALU.is_equal).then_inc(oh_b, 1)

            def cut(i):
                h = table_of(i)
                if i == 0:
                    dve.wait_ge(h_tab, NF * 4 * VK)
                else:
                    dve.wait_ge(h_ps, i)
                dve.tensor_tensor(r1[:], h, upper(h), ALU.subtract).then_inc(r1_ok, 1)
                dve.wait_ge(r1_ok, i + 1)
                dve.tensor_tensor(r2[i % 2][:], r1[:], upper(r1[:]), ALU.subtract).then_inc(r2_ok, 1)

            def centre(i):
                dve.wait_ge(h_sb, i + 1)
                dve.tensor_reduce(st[:, 0, :], H2[i % H_RING][:], AX.X, ALU.add).then_inc(ln_dve, 1)
                dve.wait_ge(ln_dve, 4 * i + 1)
                dve.scalar_tensor_tensor(out=xc[:], in0=over(st[:, 0, :], D), scalar=-1.0 / D,
                                         in1=H2[i % H_RING][:], op0=ALU.mult, op1=ALU.add).then_inc(ln_dve, 1)

            def variance(i):
                dve.wait_ge(ln_act, i + 1)
                dve.tensor_reduce(st[:, 1, :], sq[:], AX.X, ALU.add).then_inc(ln_dve, 1)

            def normalise(i):
                dve.wait_ge(ln_pool, 2 * i + 2)
                if i >= 1:
                    dve.wait_ge(nn_ready, i)
                dve.tensor_tensor(nrm[:], xc[:], over(st[:, 3, :], D), ALU.mult).then_inc(ln_dve, 1)

            def gate2(s, q):
                dve.wait_ge(l2_ps, PAIRS * s + q + 1)
                if q == 0:
                    dve.wait_ge(wb_ld[s % RING], 32 * (s // RING + 1))
                if s >= 1 and q == 0:
                    dve.wait_ge(l3_ps, s)
                dve.scalar_tensor_tensor(out=H2g[q][:], in0=two_banks(l2_bank(q)), scalar=nb2_s[:, q:q + 1],
                                         in1=WB[s % RING][:, q, :], op0=ALU.max, op1=ALU.mult).then_inc(h2_sb, 1)

            def hidden_lo(i):
                dve.wait_ge(rh_hi, i + 1)
                dve.tensor_tensor(RH[D:P, :], RF[D:P, :], RH[D:P, :].bitcast(F32), ALU.subtract)\
                   .then_inc(rh_ready, 1)

            def count_it(ins):
                ins.then_inc(rt_dve, 1)

            def then(ins, n):
                ins.then_inc(rt_dve, 1)
                dve.wait_ge(rt_dve, n)

            def rank_experts(i):
                n = RT * i
                if i == 0:
                    dve.wait_ge(cmp_zero, 1)
                dve.wait_ge(rl_ps, i + 1)
                then(dve.tensor_tensor(lg[:], PS[:, B_Y, 0:TB * E].rearrange("p (t e) -> p t e", e=E),
                                       rb2_s[:].unsqueeze(1).broadcast_to([P, TB, E]), ALU.add), n + 1)
                count_it(dve.tensor_reduce(rt[:, 0, :], lg[:], AX.X, ALU.max))
                for e in range(E):
                    if e == 2:
                        dve.wait_ge(rt_dve, n + 2)
                        count_it(dve.tensor_tensor(ex[:], lg[:], over(rt[:, 0, :], E), ALU.subtract))
                    if e > 0:
                        last = dve.tensor_tensor(cmp_[:, :, e, 0:e], lg[:, :, 0:e], over(lg[:, :, e], e), ALU.is_ge)
                    if e < E - 1:
                        last = dve.tensor_tensor(cmp_[:, :, e, e + 1:E], lg[:, :, e + 1:E],
                                                 over(lg[:, :, e], E - 1 - e), ALU.is_gt)
                then(last, n + 4)
                then(dve.tensor_reduce(rank[:], cmp_[:], AX.X, ALU.add), n + 5)
                count_it(dve.tensor_scalar(m0[:], rank[:], 0.0, None, ALU.is_equal))
                then(dve.tensor_scalar(m1[:], rank[:], 1.0, None, ALU.is_equal), n + 7)
                count_it(dve.tensor_tensor(sg[:], m0[:], m1[:], ALU.subtract))

            def two_best(i):
                n = RT * i
                dve.wait_ge(ex_act, 2 * i + 1)
                dve.wait_ge(rt_dve, n + 8)
                count_it(dve.tensor_reduce(rt[:, 1, :], ex[:], AX.X, ALU.add))
                then(dve.tensor_tensor(ps_[:], ex[:], sg[:], ALU.mult), n + 10)
                count_it(dve.tensor_reduce(rt[:, 2, :], ps_[:], AX.X, ALU.add))
                then(dve.reciprocal(rt[:, 5, :], rt[:, 1, :]), n + 12)
                count_it(dve.tensor_tensor(rt[:, 3, :], rt[:, 2, :], rt[:, 5, :], ALU.mult))

            def gates(i):
                n = RT * i
                dve.wait_ge(ex_act, 2 * i + 2)
                then(dve.tensor_scalar(rt[:, 6, :], rt[:, 4, :], 1.0, None, ALU.add), n + 14)
                then(dve.reciprocal(rt[:, 7, :], rt[:, 6, :]), n + 15)
                count_it(dve.tensor_tensor(rt[:, 5, :], rt[:, 4, :], rt[:, 7, :], ALU.mult))
                count_it(dve.tensor_tensor(g0[:], m0[:], over(rt[:, 7, :], E), ALU.mult))
                dve.wait_ge(rt_dve, n + 16)
                then(dve.tensor_tensor(g1[:], m1[:], over(rt[:, 5, :], E), ALU.mult), n + 18)
                if i >= 1:
                    dve.wait_ge(gt_ps, i)
                dve.tensor_tensor(gate[:], g0[:], g1[:], ALU.add).then_inc(gate_ready, 1)

            def result(s):
                dve.wait_ge(y_ps, s + 1)
                if s >= 2:
                    dve.wait_ge(y_st[s % 2], 16 * (s // 2))
                dve.tensor_tensor(Y[s % 2][:].rearrange("p (u j) o -> p u j o", u=2),
                                  PS[:, B_Y, :].rearrange("p (j u o) -> p u j o", u=2, o=D),
                                  H2[s % H_RING][:].rearrange("p (u j) o -> p u j o", u=2), ALU.add).then_inc(y_sb, 1)

            cut(0)
            one_hot_ids(0)
            one_hot_ids(1)
            dve.wait_ge(sel_dve, 2)
            centre(0)
            variance(0)
            cut(1)
            normalise(0)
            one_hot_ids(2)
            centre(1)
            cut(2)
            for i in range(STEPS + LAG):
                a, b, s, ahead = i < STEPS, i >= LAG, i - LAG, i + 1 < STEPS
                if ahead:
                    variance(i + 1)
                if a:
                    hidden_lo(i)
                if b:
                    gate2(s, 0)
                if ahead:
                    normalise(i + 1)
                if a:
                    rank_experts(i)
                if b:
                    gate2(s, 1)
                if a:
                    two_best(i)
                if b:
                    gate2(s, 2)
                if a:
                    gates(i)
                if i + 2 < STEPS:
                    centre(i + 2)
                if i + 3 < STEPS:
                    one_hot_ids(i + 3)
                if b:
                    result(s)


_NAMES = ("x_flat", "x_t", "consts", "tab", "wk", "wqt", "wvt", "wo", "rw1", "rb1", "rw2", "rb2",
          "w1", "b1", "w2", "b2", "w3", "b3")


def shape_constants():
    import numpy as np

    c = np.zeros((P, C_END), np.float32)
    p = np.arange(P)
    c[:, C_ID:C_ID + P] = np.eye(P)
    for k in range(VK):
        c[:, C_IOTA + k] = p + k * P
    c[p, C_MASK + (p // HEADS) % CG] = 1
    for w in range(2):
        for u in range(2):
            for z in range(2):
                for e in range(E):
                    row = 32 * w + 12 * u + 6 * z + e
                    c[(e % 2) * D:(e % 2 + 1) * D, C_SEL + (e // 2) * D + row] = 1
                    c[row, C_BM + 2 * z + u] = 1
    c[:, C_ROW:C_ROW + NV] = np.arange(NV)
    return c


def kernel(x, fside_BS_t, L0_tok_weight, L0_attn_Wq, L0_attn_Wk, L0_attn_Wv, L0_attn_Wo,
           L0_ffn_router_w1, L0_ffn_router_b1, L0_ffn_router_w2, L0_ffn_router_b2,
           L0_ffn_expert_w1, L0_ffn_expert_b1, L0_ffn_expert_w2, L0_ffn_expert_b2,
           L0_ffn_expert_w3, L0_ffn_expert_b3):
    import numpy as np
    from concourse import bacc
    from concourse.bass_utils import run_bass_kernel_spmd

    x = np.asarray(x)
    head_rows = {n: np.asarray(w).reshape(D, D, HEADS).transpose(2, 1, 0).reshape(HEADS * D, D)
                 for n, w in (("q", L0_attn_Wq), ("v", L0_attn_Wv))}
    wo = np.asarray(L0_attn_Wo).reshape(D, HEADS * D)
    b3_rows = np.zeros((D, D), np.asarray(L0_ffn_expert_b3).dtype)
    for w in range(2):
        for k in range(4):
            b3_rows[32 * w + 6 * k:32 * w + 6 * k + E] = np.asarray(L0_ffn_expert_b3)
    w1 = np.asarray(L0_ffn_expert_w1).transpose(1, 0, 2).reshape(D, E * D)
    arrays = {
        "x_flat": x.reshape(1, NB * S),
        "x_t": x.T,
        "consts": shape_constants(),
        "tab": np.asarray(L0_tok_weight).T,
        "wk": np.asarray(L0_attn_Wk).reshape(D, D, HEADS).transpose(0, 2, 1).reshape(D, HEADS * D),
        "wqt": np.concatenate([head_rows["q"]] * 2, axis=1),
        "wvt": head_rows["v"],
        "wo": np.concatenate([wo, wo]),
        "rw1": np.tile(np.asarray(L0_ffn_router_w1), (2, 4)),
        "rb1": np.tile(np.asarray(L0_ffn_router_b1), 4).reshape(P, 1),
        "rw2": np.tile(np.asarray(L0_ffn_router_w2), (4, 1)),
        "rb2": np.asarray(L0_ffn_router_b2).reshape(1, E),
        "w1": np.concatenate([w1, w1]),
        "b1": np.asarray(L0_ffn_expert_b1).reshape(PAIRS, P).T,
        "w2": np.asarray(L0_ffn_expert_w2),
        "b2": np.asarray(L0_ffn_expert_b2).reshape(PAIRS, P).T,
        "w3": np.asarray(L0_ffn_expert_w3).reshape(E * D, D),
        "b3": b3_rows,
    }
    nc = bacc.Bacc("TRN2", target_bir_lowering=False, num_devices=1)
    args = []
    for name in _NAMES:
        arrays[name] = np.ascontiguousarray(arrays[name])
        args.append(nc.dram_tensor(name, arrays[name].shape, mybir.dt.from_np(arrays[name].dtype),
                                   kind="ExternalInput").ap())
    out = nc.dram_tensor("h_out", (NB, S, D), F32, kind="ExternalOutput").ap()
    build(nc, *args, out)
    result = run_bass_kernel_spmd(nc, [arrays], core_ids=[0])
    return result.results[0]["h_out"]
```
